# Optimizing a Trainium2 kernel written in Bass

```python
import numpy as np
import jax
import jax.numpy as jnp

def _softmax(x, axis=-1):
    return jax.nn.softmax(x, axis=axis)

def _gelu(x):
    return jax.nn.gelu(x, approximate=True)

def _silu(x):
    return jax.nn.silu(x)

def _sigmoid(x):
    return jax.nn.sigmoid(x)

def _layernorm(x, axis=-1, eps=1e-05):
    m = jnp.mean(x, axis=axis, keepdims=True)
    v = jnp.var(x, axis=axis, keepdims=True)
    return (x - m) / jnp.sqrt(v + eps)

def _scatter_add(tgt, idx, src, axis=0):
    return tgt.at[idx].add(src)

def _segment_sum(src, seg, n):
    return jax.ops.segment_sum(src, seg, n)
kernel_name = 'mk_audio_tower_d1_tok_audfeat512_r4_2a58a2'

def setup_inputs(seed: int=0):
    np.random.seed(seed)
    _w = jnp.asarray

    def _rec_inputs():
        import jax
        import jax.numpy as jnp
        _rk = jax.random.key(seed)
        x = -0.000392918 + 0.999932 * jax.random.normal(jax.random.fold_in(_rk, 1), (128, 750, 32), jnp.float32)
        return x
    x = _rec_inputs()

    def _L0_tok_setup():
        import jax, jax.numpy as jnp
        import numpy as np
        PATCH_LEN = 16
        STRIDE = 8
        key = jax.random.key(seed)
        k1, k2, k3 = jax.random.split(key, 3)
        B, L, F = (128, 1024, 32)
        d_model = 128
        d_in = PATCH_LEN * F
        x = jax.random.normal(k1, (B, L, F), dtype=jnp.float32)
        W = jax.random.normal(k2, (d_in, d_model), dtype=jnp.float32) / np.sqrt(d_in)
        b = jax.random.normal(k3, (d_model,), dtype=jnp.float32) / np.sqrt(d_in)
        return {'x': x, 'W': W, 'b': b}
    _L0_tok_all = _L0_tok_setup()
    _L0_tok_in = {k: v for k, v in _L0_tok_all.items() if k in ('W', 'b')}
    del _L0_tok_all

    def _L0_attn_setup():
        import jax, jax.numpy as jnp
        import numpy as np
        B, S, D, H, E = (8, 256, 128, 8, 64)
        key = jax.random.key(seed)
        k0, k1, k2, k3, k4 = jax.random.split(key, 5)
        x = jax.random.normal(k0, (B, S, D), dtype=jnp.float32)
        Wq = jax.random.normal(k1, (H, D, E), dtype=jnp.float32) * 0.05
        Wk = jax.random.normal(k2, (H, D, E), dtype=jnp.float32) * 0.05
        Wv = jax.random.normal(k3, (H, D, D), dtype=jnp.float32) * 0.05
        Wlt = jax.random.normal(k4, (H * D, D), dtype=jnp.float32) * 0.05
        return {'x': x, 'Wq': Wq, 'Wk': Wk, 'Wv': Wv, 'Wlt': Wlt}
    _L0_attn_all = _L0_attn_setup()
    _L0_attn_in = {k: v for k, v in _L0_attn_all.items() if k in ('Wq', 'Wk', 'Wv', 'Wlt')}
    del _L0_attn_all

    def _L0_ffn_setup():
        import jax, jax.numpy as jnp
        import numpy as np
        B, S, D, F, E, K = (64, 128, 128, 512, 8, 2)
        key = jax.random.key(seed)
        k0, k1, k2, k3 = jax.random.split(key, 4)
        x = jax.random.normal(k0, (B, S, D), dtype=jnp.float32)
        Wr = jax.random.normal(k1, (D, E), dtype=jnp.float32) * D ** (-0.5)
        br = jnp.zeros((E,), dtype=jnp.float32)
        W1 = jax.random.normal(k2, (E, D, F), dtype=jnp.float32) * D ** (-0.5)
        b1 = jnp.zeros((E, F), dtype=jnp.float32)
        W2 = jax.random.normal(k3, (E, F, D), dtype=jnp.float32) * F ** (-0.5)
        b2 = jnp.zeros((E, D), dtype=jnp.float32)
        return {'x': x, 'Wr': Wr, 'br': br, 'W1': W1, 'b1': b1, 'W2': W2, 'b2': b2}
    _L0_ffn_all = _L0_ffn_setup()
    _L0_ffn_in = {k: v for k, v in _L0_ffn_all.items() if k in ('Wr', 'br', 'W1', 'b1', 'W2', 'b2')}
    del _L0_ffn_all
    return {'x': x, 'L0_tok_W': _L0_tok_in['W'], 'L0_tok_b': _L0_tok_in['b'], 'L0_attn_Wq': _L0_attn_in['Wq'], 'L0_attn_Wk': _L0_attn_in['Wk'], 'L0_attn_Wv': _L0_attn_in['Wv'], 'L0_attn_Wlt': _L0_attn_in['Wlt'], 'L0_ffn_Wr': _L0_ffn_in['Wr'], 'L0_ffn_br': _L0_ffn_in['br'], 'L0_ffn_W1': _L0_ffn_in['W1'], 'L0_ffn_b1': _L0_ffn_in['b1'], 'L0_ffn_W2': _L0_ffn_in['W2'], 'L0_ffn_b2': _L0_ffn_in['b2']}

def reference(x, L0_tok_W, L0_tok_b, L0_attn_Wq, L0_attn_Wk, L0_attn_Wv, L0_attn_Wlt, L0_ffn_Wr, L0_ffn_br, L0_ffn_W1, L0_ffn_b1, L0_ffn_W2, L0_ffn_b2):
    import jax
    import jax.numpy as jnp

    def _L0_tok_ref(x, W, b):
        import jax, jax.numpy as jnp
        import numpy as np
        PATCH_LEN = 16
        STRIDE = 8
        B, L, F = x.shape
        n_patches = (L - PATCH_LEN) // STRIDE + 1
        idx = jnp.arange(n_patches)[:, None] * STRIDE + jnp.arange(PATCH_LEN)[None, :]
        patches = x[:, idx, :]
        patches = patches.reshape(B, n_patches, PATCH_LEN * F)
        return jnp.einsum('bpk,kd->bpd', patches, W) + b

    def _L0_attn_ref(x, Wq, Wk, Wv, Wlt):
        import jax, jax.numpy as jnp
        import numpy as np
        B, S, D, H, E = (8, 256, 128, 8, 64)
        b, s, d = x.shape
        h, _, e = Wq.shape
        q = jnp.einsum('bsd,hde->bhse', x, Wq)
        k = jnp.einsum('bsd,hde->bhse', x, Wk)
        v = jnp.einsum('bsd,hdf->bhsf', x, Wv)
        s_a = jnp.einsum('bhie,bhje->bhij', k, q) / e
        attn = jax.nn.softmax(s_a, axis=-1)
        ax = jnp.einsum('bhtf,bhit->bhfi', v, attn)
        a_x = ax.transpose(0, 2, 1, 3).reshape(b, d, h * s)
        a_flat = a_x.reshape(-1, h * d)
        out = a_flat @ Wlt
        return out.reshape(b, s, d)

    def _L0_ffn_ref(x, Wr, br, W1, b1, W2, b2):
        import jax, jax.numpy as jnp
        import numpy as np
        B, S, D, F, E, K = (64, 128, 128, 512, 8, 2)
        orig_shape = x.shape
        t = x.reshape(-1, orig_shape[-1])
        logits = t @ Wr + br
        gates = jax.nn.softmax(logits, axis=-1)
        top_vals, top_idx = jax.lax.top_k(gates, K)
        top_vals = top_vals / top_vals.sum(axis=-1, keepdims=True)
        onehot = jax.nn.one_hot(top_idx, E, dtype=t.dtype)
        combine = jnp.einsum('tk,tke->te', top_vals, onehot)
        out = jnp.zeros_like(t)
        for e in range(E):
            h = jax.nn.relu(t @ W1[e] + b1[e])
            y = h @ W2[e] + b2[e]
            out = out + combine[:, e:e + 1] * y
        return out.reshape(orig_shape)
    h = _L0_tok_ref(x, L0_tok_W, L0_tok_b)
    h = h + _L0_attn_ref(_layernorm(h, axis=-1), L0_attn_Wq, L0_attn_Wk, L0_attn_Wv, L0_attn_Wlt)
    h = h + _L0_ffn_ref(_layernorm(h, axis=-1), L0_ffn_Wr, L0_ffn_br, L0_ffn_W1, L0_ffn_b1, L0_ffn_W2, L0_ffn_b2)
    return h

_drawn_inputs = setup_inputs


def setup_inputs(seed=0):
    import zlib

    import numpy as np

    out = dict(_drawn_inputs(seed))
    spreads = {'L0_ffn_br': (0.0, 0.1), 'L0_ffn_b1': (0.0, 0.1), 'L0_ffn_b2': (0.0, 0.1)}
    factors = {}
    for name, (base, spread) in spreads.items():
        noise = np.random.default_rng([zlib.crc32(name.encode()), seed]).standard_normal(out[name].shape)
        drawn = base * np.exp(spread * noise) if base else spread * noise
        out[name] = jnp.asarray(drawn.astype(out[name].dtype))
    for name, factor in factors.items():
        out[name] = (out[name] * factor).astype(out[name].dtype)
    return out
```

```python
from contextlib import ExitStack

import concourse.bass as bass
from concourse import mybir

ALU = mybir.AluOpType
ACT = mybir.ActivationFunctionType
F32 = mybir.dt.float32
F32R = mybir.dt.float32r
AX_X = mybir.AxisListType.X

P = 128
B, L, FEAT = 128, 750, 32
PATCH, STRIDE = 16, 8
S = (L - PATCH) // STRIDE + 1
D = 128
H, E = 8, 64
NE, FF = 8, 512
FC = FF // P
EPS = 1e-5
T = B * S
ROW = STRIDE * FEAT
NROW = S + 1
KC = ROW // P

GB = 4
NG = B // GB
GT = GB * S
HH = H // 2
UN = 2 * GB
LAG_T, LAG_M, LAG_V = 2, 3, 7

CT = 512
NCH = T // CT
RT = CT // P
HS = NE * FC
LAG_Y = 3
AC = H * D // P
K3 = 3 * NE
assert T % CT == 0 and GT <= 512 and HH * S == GT and H * S * D == S * H * D


def at_least(eng, sem, value):
    if isinstance(value, int) and value <= 0:
        return
    eng.wait_ge(sem, value)


def back(g, k, lag):
    k -= lag
    while k < 0:
        g, k = g - 1, k + UN
    return g, k


def exists(g):
    return not isinstance(g, int) or 0 <= g < NG


def build(nc, x, tok_w, tok_b, wq, wk, wv, wlt, wr, br, w1, b1, w2, b2, out):
    ax_dram = nc.dram_tensor("ax_scratch", (T * H * D,), F32, kind="Internal").ap()
    h_dram = nc.dram_tensor("h_scratch", (D, T), F32, kind="Internal").ap()
    ax_in = ax_dram.rearrange("(b f h i) -> b f h i", f=D, h=H, i=S)
    ax_rows = ax_dram.rearrange("(t c) -> t c", c=H * D)
    x_rows = x.rearrange("b l f -> b (l f)")

    with ExitStack() as ctx, nc.allow_non_contiguous_dma("biases once"):
        def sb(name, shape, dt=F32, stack=ctx):
            return stack.enter_context(nc.sbuf_tensor(name, shape, dt))

        def sem(name):
            return ctx.enter_context(nc.semaphore(name))

        ident = sb("ident", [P, P])
        center = sb("center", [P, P])
        average = sb("average", [P, P])
        eps = sb("eps", [P, 1])
        ones_row = sb("ones_row", [1, P])
        tokw = sb("tokw", [P, 2 * KC, D])
        tokb = sb("tokb", [D, 1])
        pair_h = sb("pair_h", [D, H, D], F32R)
        pair_l = sb("pair_l", [D, H, D], F32R)
        wvs = sb("wvs", [D, H, D])
        wlt_h = sb("wlt_h", [P, AC, D], F32R)
        wlt_l = sb("wlt_l", [P, AC, D], F32R)
        w1_h = sb("w1_h", [D, NE, FF], F32R)
        w1_l = sb("w1_l", [D, NE, FF], F32R)
        w2_h = sb("w2_h", [P, NE * FC, D], F32R)
        w2_l = sb("w2_l", [P, NE * FC, D], F32R)
        b1s = sb("b1s", [P, NE * FC])
        wrs = sb("wrs", [D, NE])
        brs = sb("brs", [1, NE])
        b2raw = sb("b2raw", [NE, D])
        b2_h = sb("b2_h", [NE, D], F32R)
        b2_l = sb("b2_l", [NE, D], F32R)
        b2_3 = sb("b2_3", [K3, D], F32R)
        pick = sb("pick", [K3, NE, P], F32R)
        rank = sb("rank", [P, RT, NE])

        first = ExitStack()
        xin = sb("xin", [NROW, 2, GB, ROW], stack=first)
        xT = sb("xT", [P, KC, GB, NROW], stack=first)
        hT = sb("hT", [D, GT], stack=first)
        sqA = sb("sqA", [D, GT], stack=first)
        stdA = sb("stdA", [D, GT], stack=first)
        rstdA = sb("rstdA", [D, GT], stack=first)
        xnT = sb("xnT", [D, 2, GT], stack=first)
        xn_h = sb("xn_h", [D, GT], F32R, stack=first)
        xn_l = sb("xn_l", [D, GT], F32R, stack=first)
        xn = sb("xn", [S, 2, GB, D], stack=first)
        z = sb("z", [D, 2, GB, H, S], stack=first)
        peak = sb("peak", [S, 2, HH], stack=first)
        cent = sb("cent", [S, 2, HH, S], stack=first)
        expo = sb("expo", [S, 2, HH, S], stack=first)
        total = sb("total", [S, 2, HH], stack=first)
        inv = sb("inv", [S, 2, HH], stack=first)
        prob = sb("prob", [S, 2, HH, S], stack=first)
        probT = sb("probT", [S, 2, HH, S], stack=first)
        mix = sb("mix", [D, H, GB, S], stack=first)
        val = sb("val", [D, 2, GB, HH, S], stack=first)
        raw = sb("raw", [P, 4096], stack=first)
        first.close()

        second = ExitStack()
        arow = sb("arow", [P, 2, RT, H * D], stack=second)
        hch = sb("hch", [D, 2, CT], stack=second)
        aT_h = sb("aT_h", [P, 2, CT], F32R, stack=second)
        aT_l = sb("aT_l", [P, 2, CT], F32R, stack=second)
        h1 = sb("h1", [D, 2, CT], stack=second)
        sqB = sb("sqB", [D, CT], stack=second)
        stdB = sb("stdB", [D, CT], stack=second)
        rstdB = sb("rstdB", [D, CT], stack=second)
        tT = sb("tT", [D, CT], stack=second)
        t_h = sb("t_h", [D, 2, CT], F32R, stack=second)
        t_l = sb("t_l", [D, 2, CT], F32R, stack=second)
        lg = sb("lg", [P, RT, NE], stack=second)
        eq = sb("eq", [P, RT, NE], stack=second)
        key = sb("key", [P, RT, NE], stack=second)
        one1 = sb("one1", [P, RT, NE], stack=second)
        one2 = sb("one2", [P, RT, NE], stack=second)
        comb = sb("comb", [P, RT, NE], stack=second)
        top = sb("top", [P, 8, RT], stack=second)
        comb3 = sb("comb3", [P, RT, K3], F32R, stack=second)
        combT = sb("combT", [K3, 2, CT], F32R, stack=second)
        gate = sb("gate", [P, 2, CT], stack=second)
        hid = sb("hid", [P, 2, CT], stack=second)
        hid_h = sb("hid_h", [P, 4, CT], F32R, stack=second)
        hid_l = sb("hid_l", [P, 4, CT], F32R, stack=second)
        gated = sb("gated", [D, 2, CT], stack=second)
        acc = sb("acc", [D, 2, CT], stack=second)
        osb = sb("osb", [P, 2, RT, D], stack=second)
        second.close()

        bank = [ctx.enter_context(nc.psum_tensor(f"bank{i}", [P, 512], F32)) for i in range(8)]
        front_ps, score_ps, probT_ps, mix_ps, val_ps = bank[0:2], bank[2:4], bank[4:6], bank[6], bank[7]
        turn_ps, proj_ps, hid_ps, y_ps, gate_ps = bank[0:2], bank[2], bank[3:5], bank[5:7], bank[7]

        ws_small, ws_tok, ws_qk, ws_v, ws_lt, ws_1, ws_2 = (sem(n) for n in (
            "ws_small", "ws_tok", "ws_qk", "ws_v", "ws_lt", "ws_1", "ws_2"))
        cs = sem("cs")
        qkT_done, qkT_kept, pair_done, pair_kept = (sem(n) for n in ("qkT_done", "qkT_kept", "pair_done", "pair_kept"))
        split_lt, split_12, split_b2, b2_moved = (sem(n) for n in ("split_lt", "split_12", "split_b2", "b2_moved"))
        x_in = [sem("x_in0"), sem("x_in1")]
        xT_done, xT_kept, h_done, h_kept, h_out = (sem(n) for n in ("xT_done", "xT_kept", "h_done", "h_kept", "h_out"))
        hc_done, sq_kept, var_done, std_kept, rstd_kept = (sem(n) for n in (
            "hc_done", "sq_kept", "var_done", "std_kept", "rstd_kept"))
        xnT_kept, xnh_kept, xnl_kept, xn_done, xn_kept = (sem(n) for n in (
            "xnT_kept", "xnh_kept", "xnl_kept", "xn_done", "xn_kept"))
        z_done, z_kept = sem("z_done"), sem("z_kept")
        score_done, peak_kept, cent_kept, exp_kept, total_kept, inv_kept = (sem(n) for n in (
            "score_done", "peak_kept", "cent_kept", "exp_kept", "total_kept", "inv_kept"))
        prob_kept, probT_done, probT_kept = sem("prob_kept"), sem("probT_done"), sem("probT_kept")
        mix_done, mix_kept, val_done, val_kept = (sem(n) for n in ("mix_done", "mix_kept", "val_done", "val_kept"))
        val_out = [sem("val_out0"), sem("val_out1")]
        a_in = [sem("a_in0"), sem("a_in1")]
        aT_done, aTh_kept, aTl_kept, proj_done, h1_kept = (sem(n) for n in (
            "aT_done", "aTh_kept", "aTl_kept", "proj_done", "h1_kept"))
        hc2_done, sq2_kept, var2_done, std2_kept, rstd2_kept, t_kept, th_kept, tl_kept = (sem(n) for n in (
            "hc2_done", "sq2_kept", "var2_done", "std2_kept", "rstd2_kept", "t_kept", "th_kept", "tl_kept"))
        lg_done, route, gap_kept, gapexp_kept, comb_kept, combT_done, combT_kept = (sem(n) for n in (
            "lg_done", "route", "gap_kept", "gapexp_kept", "comb_kept", "combT_done", "combT_kept"))
        bias_done, acc_begun, gate_done, gate_kept = (sem(n) for n in ("bias_done", "acc_begun", "gate_done", "gate_kept"))
        hid_done, hid_kept, hidh_kept, hidl_kept, used = (sem(n) for n in (
            "hid_done", "hid_kept", "hidh_kept", "hidl_kept", "used"))
        gated_kept, acc_kept, outT_done, out_kept = (sem(n) for n in ("gated_kept", "acc_kept", "outT_done", "out_kept"))
        out_sent = [sem("out_sent0"), sem("out_sent1")]

        block = ctx.enter_context(nc.Block())
        mm = nc.tensor.matmul

        def three(dst, wh, wl, vh, vl, start, stop):
            mm(dst, wh, vh, start=start, stop=False)
            mm(dst, wh, vl, start=False, stop=False)
            return mm(dst, wl, vh, start=False, stop=stop)

        def steps_first(eng, step):
            for g in (0, 1):
                for k in range(UN):
                    step(g, k, 0, g)
            with eng.Fori(1, NG // 2 - 1) as i:
                for q in (0, 1):
                    for k in range(UN):
                        step(2 * i + q, k, i, q)
            for g in (NG - 2, NG - 1):
                for k in range(UN):
                    step(g, k, NG // 2 - 1, g % 2)
            for k in range(LAG_V):
                step(NG, k, NG // 2, 0)

        def steps_second(eng, chunk):
            chunk(0, 0, 0, True)
            chunk(1, 0, 1, True)
            chunk(2, 1, 0, True)
            with eng.Fori(1, (NCH - 3) // 2) as i:
                chunk(2 * i + 1, i, 1, True)
                chunk(2 * i + 2, i + 1, 0, True)
            chunk(NCH - 2, (NCH - 3) // 2, 1, True)
            chunk(NCH - 1, (NCH - 1) // 2, 0, False)

        def first_part_over(eng):
            eng.wait_ge(h_out, 16 * NG)
            for half in (0, 1):
                eng.wait_ge(val_out[half], 16 * NG)

        @block.sync
        def _(sp):
            sp.dma_start(tokw[:], tok_w.rearrange("(c p) d -> p c d", p=P)).then_inc(ws_tok, 16)
            sp.dma_start(raw[:, 0:H * E], wq.rearrange("h d e -> d h e")).then_inc(ws_qk, 16)
            sp.dma_start(raw[:, H * E:2 * H * E], wk.rearrange("h d e -> d h e")).then_inc(ws_qk, 16)
            sp.dma_start(wvs[:], wv.rearrange("h d f -> d h f")).then_inc(ws_v, 16)

            def load_x(g, i, q):
                at_least(sp, xT_done, KC * (g - 1))
                if isinstance(g, int):
                    src = x_rows[g * GB:(g + 1) * GB, 0:NROW * ROW]
                else:
                    src = x_rows[bass.ds(g * GB, GB), 0:NROW * ROW]
                sp.dma_start(xin[:, q], src.rearrange("b (r c) -> r b c", c=ROW)).then_inc(x_in[q], 16)

            def store_h(g):
                at_least(sp, h_kept, g + 1)
                dst = h_dram[:, g * GT:(g + 1) * GT] if isinstance(g, int) else h_dram[:, bass.ds(g * GT, GT)]
                sp.dma_start(dst, hT[:]).then_inc(h_out, 16)

            load_x(0, 0, 0)
            load_x(1, 0, 1)
            store_h(0)

            def step(g, k, i, q):
                nxt = g + 1
                if k == 2 and exists(g + 2):
                    load_x(g + 2, i + 1, q)
                if k == 3 and exists(nxt):
                    store_h(nxt)
                gv, h = back(g, k, LAG_V)
                if h % HH == HH - 1 and exists(gv):
                    half = h // HH
                    at_least(sp, val_kept, H * gv + h + 1)
                    dst = ax_in[gv * GB:(gv + 1) * GB] if isinstance(gv, int) else ax_in[bass.ds(gv * GB, GB)]
                    sp.dma_start(dst[:, :, half * HH:(half + 1) * HH, :].rearrange("b f h i -> f b (h i)"),
                                 val[:, half].rearrange("f b h i -> f b (h i)")).then_inc(val_out[half], 16)

            steps_first(sp, step)

            first_part_over(sp)

            def load_a(c, i, q):
                at_least(sp, aT_done, AC * (c - 1))
                at_least(sp, h1_kept, c - 1)
                if isinstance(c, int):
                    rows, cols = ax_rows[c * CT:(c + 1) * CT, :], h_dram[:, c * CT:(c + 1) * CT]
                else:
                    rows, cols = ax_rows[bass.ds(c * CT, CT), :], h_dram[:, bass.ds(c * CT, CT)]
                sp.dma_start(arow[:, q], rows.rearrange("(r p) n -> p r n", p=P)).then_inc(a_in[q], 16)
                sp.dma_start(hch[:, q], cols).then_inc(a_in[q], 16)

            def store_out(c, q):
                at_least(sp, out_kept, c + 1)
                dst = out[c * CT:(c + 1) * CT, :] if isinstance(c, int) else out[bass.ds(c * CT, CT), :]
                sp.dma_start(dst.rearrange("(r p) d -> p r d", p=P), osb[:, q]).then_inc(out_sent[q], 16)

            load_a(0, 0, 0)
            load_a(1, 0, 1)

            def chunk(c, i, q, more):
                if not isinstance(c, int) or c > 0:
                    store_out(c - 1, 1 - q)
                if not isinstance(c, int) or c + 2 < NCH:
                    load_a(c + 2, i + 1, q)

            steps_second(sp, chunk)
            store_out(NCH - 1, (NCH - 1) % 2)
            sp.wait_ge(out_sent[0], 16 * ((NCH + 1) // 2))
            sp.wait_ge(out_sent[1], 16 * (NCH // 2))

        @block.gpsimd
        def _(pool):
            count = [0]

            def const(ins):
                count[0] += 1
                ins.then_inc(cs, 1)
                return count[0]

            const(pool.memset(ident[:], 0.0))
            const(pool.memset(average[:], 1.0 / D))
            const(pool.memset(center[:], -1.0 / D))
            const(pool.memset(eps[:], EPS))
            const(pool.memset(ones_row[:], 1.0))
            pool.wait_ge(cs, count[0])
            const(pool.affine_select(out=ident[:], in_=ident[:], compare_op=ALU.not_equal, fill=1.0, base=0,
                                     pattern=[[-1, P]], channel_multiplier=1))
            const(pool.affine_select(out=center[:], in_=center[:], compare_op=ALU.not_equal, fill=1.0 - 1.0 / D,
                                     base=0, pattern=[[-1, P]], channel_multiplier=1))
            assert count[0] == 7
            for e in range(NE):
                const(pool.memset(rank[:, :, e:e + 1], float(NE - e)))
            pool.wait_ge(pair_kept, 1)
            grid = raw[0:K3, 0:NE * P].rearrange("k (e p) -> k e p", e=NE)
            pool.wait_ge(cs, const(pool.memset(grid, 0.0)))
            for row in (0, NE):
                pool.wait_ge(cs, const(pool.affine_select(
                    out=grid, in_=grid, compare_op=ALU.not_equal, fill=1.0, base=-row,
                    pattern=[[-1, NE], [0, P]], channel_multiplier=1)))
            pool.wait_ge(cs, const(pool.tensor_copy(pick[:], grid)))
            pool.wait_ge(split_lt, 2)
            pool.dma_start(raw[:], w1.rearrange("e d f -> d e f")).then_inc(ws_1, 16)

            def split(src, high, low, n):
                pool.tensor_copy(high, src).then_inc(split_12, 1)
                pool.wait_ge(split_12, n)
                pool.tensor_tensor(low, src, high.bitcast(F32), ALU.subtract).then_inc(split_12, 1)

            def scale_prob(g, k):
                n = UN * g + k
                at_least(pool, inv_kept, n + 1)
                at_least(pool, exp_kept, n + 1)
                at_least(pool, probT_done, n - 1)
                nc.gpsimd.tensor_tensor(prob[:, k % 2], expo[:, k % 2],
                                        inv[:, k % 2].unsqueeze(2).to_broadcast([S, HH, S]), ALU.mult).then_inc(prob_kept, 1)

            def low_xn(g, q):
                at_least(pool, xnh_kept, g + 1)
                at_least(pool, z_done, H * g)
                nc.gpsimd.tensor_tensor(xn_l[:], xnT[:, q], xn_h[:].bitcast(F32), ALU.subtract).then_inc(xnl_kept, 1)

            low_xn(0, 0)
            state = {"w": 0}

            def step(g, k, i, q):
                if k == 2 and exists(g + 1):
                    low_xn(g + 1, 1 - q)
                if exists(g):
                    scale_prob(g, k)
                if isinstance(g, int) and g in (0, 1) and k in (1, 3, 5, 7):
                    j = (k - 1) // 2
                    sl = slice(j * 1024, (j + 1) * 1024)
                    src = raw[:, sl]
                    if g == 0:
                        if k == 1:
                            pool.wait_ge(ws_1, 16)
                        hi, lo = w1_h, w1_l
                    else:
                        if k == 1:
                            pool.wait_ge(ws_2, 16)
                        hi, lo = w2_h, w2_l
                    hi, lo = hi[:].rearrange("p a b -> p (a b)")[:, sl], lo[:].rearrange("p a b -> p (a b)")[:, sl]
                    state["w"] += 2
                    split(src, hi, lo, state["w"] - 1)
                    if g == 0 and k == 7:
                        pool.wait_ge(split_12, state["w"])
                        pool.dma_start(raw[:], w2.rearrange("e (c p) d -> p (e c) d", p=P)).then_inc(ws_2, 16)

            steps_first(pool, step)

            first_part_over(pool)

            def low_t(c, q):
                at_least(pool, th_kept, c + 1)
                at_least(pool, used, HS * (c - 1))
                nc.gpsimd.tensor_tensor(t_l[:, q], tT[:], t_h[:, q].bitcast(F32), ALU.subtract).then_inc(tl_kept, 1)

            low_t(0, 0)

            def chunk(c, i, q, more):
                for s in range(HS + LAG_Y + 2):
                    if s < HS:
                        n = HS * c + s
                        at_least(pool, hidh_kept, n + 1)
                        at_least(pool, used, n - 3)
                        nc.gpsimd.tensor_tensor(hid_l[:, s % 4], hid[:, s % 2], hid_h[:, s % 4].bitcast(F32),
                                                ALU.subtract).then_inc(hidl_kept, 1)
                    if s == 24 and more:
                        low_t(c + 1, 1 - q)
                    if s >= FC + LAG_Y + 1 and (s - LAG_Y - 1) % FC == 0 or s == HS + LAG_Y + 1:
                        e = min((s - LAG_Y - 1) // FC - 1, NE - 1)
                        m = NE * c + e
                        at_least(pool, gated_kept, m + 1)
                        if e == 0:
                            at_least(pool, acc_begun, c + 1)
                        at_least(pool, acc_kept, m)
                        nc.gpsimd.tensor_tensor(acc[:, q], acc[:, q], gated[:, e % 2], ALU.add).then_inc(acc_kept, 1)

            steps_second(pool, chunk)

        @block.scalar
        def _(act):
            A = nc.scalar.activation
            act.dma_start(tokb[:], tok_b.rearrange("(d o) -> d o", o=1)).then_inc(ws_small, 16)
            act.dma_start(b1s[:], b1.rearrange("e (c p) -> p (e c)", p=P)).then_inc(ws_small, 16)
            act.dma_start(wrs[:], wr).then_inc(ws_small, 16)
            act.dma_start(brs[:], br.rearrange("(o e) -> o e", o=1)).then_inc(ws_small, 16)
            act.dma_start(b2raw[:], b2).then_inc(ws_small, 16)
            act.dma_start(raw[:, 2 * H * E:2 * H * E + AC * D], wlt.rearrange("(c p) d -> p c d", p=P)).then_inc(ws_lt, 16)
            act.wait_ge(ws_small, 5 * 16)
            act.wait_ge(cs, 7)
            act.wait_ge(split_b2, 2)
            for j, part in enumerate((b2_h, b2_h, b2_l)):
                act.dma_start(b2_3[j * NE:(j + 1) * NE, :].bitcast(F32), part[:].bitcast(F32)).then_inc(b2_moved, 16)

            def keep_xT(g, c):
                at_least(act, xT_done, KC * g + c + 1)
                at_least(act, h_done, g)
                A(xT[:, c], front_ps[c][:, 0:GB * NROW].rearrange("p (b r) -> p b r", b=GB), ACT.Copy).then_inc(xT_kept, 1)

            def keep_h(g):
                at_least(act, h_done, g + 1)
                at_least(act, hc_done, g)
                at_least(act, h_out, 16 * g)
                A(hT[:], front_ps[0][:, 0:GT], ACT.Identity, bias=tokb[:]).then_inc(h_kept, 1)

            def keep_sq(g):
                at_least(act, hc_done, g + 1)
                at_least(act, var_done, g)
                A(sqA[:], front_ps[1][:, 0:GT], ACT.Square).then_inc(sq_kept, 1)

            def keep_std(g):
                at_least(act, var_done, g + 1)
                at_least(act, rstd_kept, g)
                A(stdA[:], front_ps[0][:, 0:GT], ACT.Sqrt, bias=eps[:]).then_inc(std_kept, 1)

            def keep_xnh(g, q):
                at_least(act, xnT_kept, g + 1)
                at_least(act, z_done, H * g)
                at_least(act, xnl_kept, g)
                A(xn_h[:], xnT[:, q], ACT.Copy).then_inc(xnh_kept, 1)

            for c in range(KC):
                keep_xT(0, c)
            keep_h(0)
            keep_sq(0)
            keep_std(0)
            keep_xnh(0, 0)

            def step(g, k, i, q):
                more = exists(g + 1)
                if k == 0 and more:
                    for c in range(KC):
                        keep_xT(g + 1, c)
                if k == 1 and more:
                    keep_h(g + 1)
                if k == 2 and more:
                    keep_std(g + 1)
                gv, h = back(g, k, LAG_V)
                if exists(gv):
                    a = H * gv + h
                    half = h // HH
                    at_least(act, val_done, a + 1)
                    if h % HH == 0:
                        at_least(act, val_out[half], 16 * gv)
                    A(val[:, half, :, h % HH, :], val_ps[:, 0:GT].rearrange("f (b i) -> f b i", b=GB),
                      ACT.Copy).then_inc(val_kept, 1)
                if exists(g):
                    n = UN * g + k
                    at_least(act, cent_kept, n + 1)
                    at_least(act, prob_kept, n - 1)
                    A(expo[:, k % 2], cent[:, k % 2], ACT.Exp, scale=1.0 / E).then_inc(exp_kept, 1)
                if k == 1 and more:
                    keep_sq(g + 1)
                if k == 2 and more:
                    keep_xnh(g + 1, 1 - q)
                gt, kt = back(g, k, LAG_T)
                if exists(gt):
                    n = UN * gt + kt
                    at_least(act, probT_done, n + 1)
                    at_least(act, mix_done, n - 1)
                    A(probT[:, kt % 2], probT_ps[kt % 2][0:S, 0:GT].rearrange("j (h i) -> j h i", h=HH),
                      ACT.Copy).then_inc(probT_kept, 1)
                gm, km = back(g, k, LAG_M)
                if exists(gm):
                    n = UN * gm + km
                    half, b = km // GB, km % GB
                    at_least(act, mix_done, n + 1)
                    at_least(act, val_done, H * gm + HH * half - HH)
                    A(mix[:, half * HH:(half + 1) * HH, b, :],
                      mix_ps[:, 0:GT].rearrange("d (h i) -> d h i", h=HH), ACT.Copy).then_inc(mix_kept, 1)

            steps_first(act, step)

            first_part_over(act)

            def keep_aTh(c, j):
                m = AC * c + j
                at_least(act, aT_done, m + 1)
                at_least(act, proj_done, m - 1)
                A(aT_h[:, j % 2], turn_ps[j % 2][:], ACT.Copy).then_inc(aTh_kept, 1)

            def keep_sq2(c):
                at_least(act, hc2_done, c + 1)
                at_least(act, var2_done, c)
                A(sqB[:], turn_ps[0][:], ACT.Square).then_inc(sq2_kept, 1)

            def keep_std2(c):
                at_least(act, var2_done, c + 1)
                at_least(act, rstd2_kept, c)
                A(stdB[:], turn_ps[1][:], ACT.Sqrt, bias=eps[:]).then_inc(std2_kept, 1)

            def keep_th(c, q):
                at_least(act, t_kept, c + 1)
                at_least(act, used, HS * (c - 1))
                A(t_h[:, q], tT[:], ACT.Copy).then_inc(th_kept, 1)

            def keep_gapexp(c):
                at_least(act, gap_kept, c + 1)
                A(top[:, 3], top[:, 2], ACT.Exp).then_inc(gapexp_kept, 1)

            def keep_combT(c, q):
                at_least(act, combT_done, c + 1)
                at_least(act, gate_done, NE * (c - 1))
                A(combT[:, q], turn_ps[1][0:K3, :], ACT.Copy).then_inc(combT_kept, 1)

            def keep_out(c, q):
                at_least(act, outT_done, c + 1)
                if not isinstance(c, int):
                    act.wait_ge(out_sent[q], 8 * (c - q))
                else:
                    at_least(act, out_sent[q], 16 * (c // 2))
                A(osb[:, q], proj_ps[:].rearrange("p (r d) -> p r d", r=RT), ACT.Copy).then_inc(out_kept, 1)

            for j in range(AC):
                keep_aTh(0, j)
            keep_sq2(0)
            keep_std2(0)
            keep_th(0, 0)
            keep_gapexp(0)
            keep_combT(0, 0)

            def chunk(c, i, q, more):
                for s in range(HS):
                    n = HS * c + s
                    at_least(act, hid_kept, n + 1)
                    at_least(act, used, n - 3)
                    A(hid_h[:, s % 4], hid[:, s % 2], ACT.Copy).then_inc(hidh_kept, 1)
                    if s == 2 and (not isinstance(c, int) or c > 0):
                        keep_out(c - 1, 1 - q)
                    if s % FC == 1:
                        e = s // FC
                        m = NE * c + e
                        at_least(act, gate_done, m + 1)
                        at_least(act, gated_kept, m - 1)
                        A(gate[:, e % 2], gate_ps[:], ACT.Copy).then_inc(gate_kept, 1)
                    if more:
                        if s % 2 == 0 and s < 2 * AC:
                            keep_aTh(c + 1, s // 2)
                        if s == 19:
                            keep_sq2(c + 1)
                        if s == 21:
                            keep_std2(c + 1)
                        if s == 23:
                            keep_th(c + 1, 1 - q)
                        if s == 26:
                            keep_gapexp(c + 1)
                        if s == 30:
                            keep_combT(c + 1, 1 - q)

            steps_second(act, chunk)
            keep_out(NCH - 1, (NCH - 1) % 2)

        @block.vector
        def _(dve):
            V = nc.vector
            dve.wait_ge(ws_small, 5 * 16)
            V.tensor_copy(b2_h[:], b2raw[:]).then_inc(split_b2, 1)
            dve.wait_ge(split_b2, 1)
            V.tensor_tensor(b2_l[:], b2raw[:], b2_h[:].bitcast(F32), ALU.subtract).then_inc(split_b2, 1)
            dve.wait_ge(ws_lt, 16)
            lt = raw[:, 2 * H * E:2 * H * E + AC * D].rearrange("p (c d) -> p c d", c=AC)
            V.tensor_copy(wlt_h[:], lt).then_inc(split_lt, 1)
            dve.wait_ge(split_lt, 1)
            V.tensor_tensor(wlt_l[:], lt, wlt_h[:].bitcast(F32), ALU.subtract).then_inc(split_lt, 1)
            for j in range(4):
                dve.wait_ge(qkT_done, j + 1)
                V.tensor_copy(raw[0:E, 2048 + 512 * j:2048 + 512 * (j + 1)], bank[j][0:E, :]).then_inc(qkT_kept, 1)
            for j in range(2):
                dve.wait_ge(pair_done, j + 1)
                src = bank[4 + j][:].rearrange("p (h d) -> p h d", h=4)
                V.tensor_copy(pair_h[:, 4 * j:4 * j + 4], src).then_inc(qkT_kept, 1)
                dve.wait_ge(qkT_kept, 5 + j)
                ins = V.tensor_tensor(pair_l[:, 4 * j:4 * j + 4], src, pair_h[:, 4 * j:4 * j + 4].bitcast(F32),
                                      ALU.subtract)
            ins.then_inc(pair_kept, 1)

            def keep_rstd(g, q):
                at_least(dve, std_kept, g + 1)
                at_least(dve, xnT_kept, g)
                V.reciprocal(rstdA[:], stdA[:]).then_inc(rstd_kept, 1)
                at_least(dve, rstd_kept, g + 1)
                at_least(dve, score_done, UN * (g - 1))
                V.tensor_tensor(xnT[:, q], front_ps[1][:, 0:GT], rstdA[:], ALU.mult).then_inc(xnT_kept, 1)

            def keep_xn(g, q):
                at_least(dve, xn_done, g + 1)
                at_least(dve, mix_done, UN * (g - 1))
                V.tensor_copy(xn[:, q], front_ps[1][0:S, :].rearrange("t (b d) -> t b d", b=GB)).then_inc(xn_kept, 1)

            def keep_z(g, h, q):
                at_least(dve, z_done, H * g + h + 1)
                at_least(dve, score_done, UN * (g - 1))
                V.tensor_copy(z[:, q, :, h, :],
                              front_ps[h % 2][:, 0:GT].rearrange("d (b j) -> d b j", b=GB)).then_inc(z_kept, 1)

            keep_rstd(0, 0)
            keep_xn(0, 0)
            for h in range(H):
                keep_z(0, h, 0)

            Z_AT = {3: (0,), 4: (1, 2), 5: (3, 4), 6: (5, 6), 7: (7,)}

            def step(g, k, i, q):
                if exists(g):
                    n = UN * g + k
                    sc = score_ps[k % 2][0:S, 0:GT].rearrange("i (h j) -> i h j", h=HH)
                    at_least(dve, score_done, n + 1)
                    V.tensor_reduce(peak[:, k % 2], sc, AX_X, ALU.max).then_inc(peak_kept, 1)
                    at_least(dve, peak_kept, n + 1)
                    at_least(dve, exp_kept, n - 1)
                    V.tensor_tensor(cent[:, k % 2], sc, peak[:, k % 2].unsqueeze(2).to_broadcast([S, HH, S]),
                                    ALU.subtract).then_inc(cent_kept, 1)
                if exists(g + 1):
                    if k == 2:
                        keep_rstd(g + 1, 1 - q)
                    if k == 3:
                        keep_xn(g + 1, 1 - q)
                    for h in Z_AT.get(k, ()):
                        keep_z(g + 1, h, 1 - q)
                if exists(g):
                    at_least(dve, exp_kept, n + 1)
                    V.tensor_reduce(total[:, k % 2], expo[:, k % 2], AX_X, ALU.add).then_inc(total_kept, 1)
                    at_least(dve, total_kept, n + 1)
                    at_least(dve, prob_kept, n - 1)
                    V.reciprocal(inv[:, k % 2], total[:, k % 2]).then_inc(inv_kept, 1)

            steps_first(dve, step)

            first_part_over(dve)

            def keep_aTl(c, j):
                at_least(dve, aTh_kept, AC * c + j + 1)
                at_least(dve, proj_done, AC * c + j - 1)
                V.tensor_tensor(aT_l[:, j % 2], turn_ps[j % 2][:], aT_h[:, j % 2].bitcast(F32),
                                ALU.subtract).then_inc(aTl_kept, 1)

            def keep_h1(c, i, q):
                at_least(dve, proj_done, AC * (c + 1))
                if isinstance(c, int):
                    dve.wait_ge(a_in[q], 32 * (c // 2 + 1))
                else:
                    dve.wait_ge(a_in[q], 16 * (c - q + 2))
                at_least(dve, acc_begun, c - 1)
                V.tensor_tensor(h1[:, q], proj_ps[:], hch[:, q], ALU.add).then_inc(h1_kept, 1)

            def keep_t(c):
                at_least(dve, std2_kept, c + 1)
                V.reciprocal(rstdB[:], stdB[:]).then_inc(rstd2_kept, 1)
                at_least(dve, rstd2_kept, c + 1)
                at_least(dve, lg_done, c)
                at_least(dve, tl_kept, c)
                V.tensor_tensor(tT[:], turn_ps[0][:], rstdB[:], ALU.mult).then_inc(t_kept, 1)

            NR = 19

            def routing(c):
                at_least(dve, lg_done, c + 1)
                at_least(dve, combT_done, c)
                step_no = [0]

                def link(ins):
                    step_no[0] += 1
                    ins.then_inc(route, 1)
                    dve.wait_ge(route, NR * c + step_no[0])

                wide = lambda a: a.unsqueeze(2).to_broadcast([P, RT, NE])
                link(V.tensor_copy(lg[:], turn_ps[1][:, 0:RT * NE].rearrange("p (r e) -> p r e", r=RT)))
                for which, one, m, kk in ((0, one1, top[:, 0], top[:, 4]), (1, one2, top[:, 1], top[:, 5])):
                    link(V.tensor_reduce(m, lg[:], AX_X, ALU.max))
                    link(V.tensor_tensor(eq[:], lg[:], wide(m), ALU.is_equal))
                    link(V.tensor_tensor(key[:], eq[:], rank[:], ALU.mult))
                    link(V.tensor_reduce(kk, key[:], AX_X, ALU.max))
                    link(V.tensor_tensor(one[:], rank[:], wide(kk), ALU.is_equal))
                    if which == 0:
                        link(V.scalar_tensor_tensor(lg[:], one[:], -3.0e38, lg[:], ALU.mult, ALU.add))
                V.tensor_tensor(top[:, 2], top[:, 1], top[:, 0], ALU.subtract).then_inc(gap_kept, 1)
                at_least(dve, gapexp_kept, c + 1)
                link(V.tensor_scalar(top[:, 6], top[:, 3], 1.0, None, ALU.add))
                link(V.reciprocal(top[:, 7], top[:, 6]))
                link(V.tensor_tensor(top[:, 6], top[:, 7], top[:, 3], ALU.mult))
                link(V.tensor_tensor(comb[:], one1[:], wide(top[:, 7]), ALU.mult))
                link(V.tensor_tensor(key[:], one2[:], wide(top[:, 6]), ALU.mult))
                link(V.tensor_tensor(comb[:], comb[:], key[:], ALU.add))
                link(V.tensor_copy(comb3[:, :, 0:NE], comb[:]))
                V.tensor_copy(comb3[:, :, 2 * NE:K3], comb[:]).then_inc(comb_kept, 1)
                V.tensor_tensor(comb3[:, :, NE:2 * NE], comb[:], comb3[:, :, 0:NE].bitcast(F32),
                                ALU.subtract).then_inc(comb_kept, 1)
                assert step_no[0] == NR, step_no

            for j in range(AC):
                keep_aTl(0, j)
            keep_h1(0, 0, 0)
            keep_t(0)
            routing(0)

            def chunk(c, i, q, more):
                for s in range(HS + LAG_Y + 1):
                    if s < HS:
                        n = HS * c + s
                        at_least(dve, hid_done, n + 1)
                        at_least(dve, hidl_kept, n - 1)
                        V.tensor_scalar(hid[:, s % 2], hid_ps[s % 2][:], b1s[:, s:s + 1], 0.0,
                                        ALU.add, ALU.max).then_inc(hid_kept, 1)
                    if s == 1:
                        at_least(dve, bias_done, c + 1)
                        at_least(dve, outT_done, c - 1)
                        V.tensor_tensor(acc[:, q], gate_ps[:], h1[:, q], ALU.add).then_inc(acc_begun, 1)
                    if s >= LAG_Y + FC and (s - LAG_Y) % FC == 0:
                        e = (s - LAG_Y) // FC - 1
                        m = NE * c + e
                        at_least(dve, gate_kept, m + 1)
                        at_least(dve, used, HS * c + FC * (e + 1))
                        at_least(dve, acc_kept, m - 1)
                        V.tensor_tensor(gated[:, e % 2], y_ps[e % 2][:], gate[:, e % 2], ALU.mult).then_inc(gated_kept, 1)
                    if more:
                        if s % 2 == 0 and s < 2 * AC:
                            keep_aTl(c + 1, s // 2)
                        if s == 18:
                            keep_h1(c + 1, i, 1 - q)
                        if s == 22:
                            keep_t(c + 1)
                        if s == 26:
                            routing(c + 1)

            steps_second(dve, chunk)

        @block.tensor
        def _(pe):
            pe.wait_ge(cs, 7)
            pe.wait_ge(ws_qk, 32)
            for j in range(4):
                for m in range(4):
                    o = (4 * j + m) * E
                    ins = nc.tensor.transpose(bank[j][0:E, m * D:(m + 1) * D], raw[:, o:o + E], ident[:])
                ins.then_inc(qkT_done, 1)
            pe.wait_ge(qkT_kept, 4)
            for j in range(2):
                for m in range(4):
                    h = 4 * j + m
                    qT = raw[0:E, 2048 + h * D:2048 + (h + 1) * D]
                    kT = raw[0:E, 2048 + (H + h) * D:2048 + (H + h + 1) * D]
                    ins = mm(bank[4 + j][:, m * D:(m + 1) * D], qT, kT, start=True, stop=True)
                ins.then_inc(pair_done, 1)
            pe.wait_ge(pair_kept, 1)
            pe.wait_ge(ws_tok, 16)
            pe.wait_ge(ws_v, 16)

            def turn_x(g, c, i, q):
                at_least(pe, z_kept, H * g)
                if c == 0:
                    at_least(pe, x_in[q], 16 * (i + 1))
                for b in range(GB):
                    ins = nc.tensor.transpose(front_ps[c][:, b * NROW:(b + 1) * NROW],
                                              xin[:, q, b, c * P:(c + 1) * P], ident[0:NROW, 0:NROW])
                ins.then_inc(xT_done, 1)

            def embed(g):
                at_least(pe, xT_kept, KC * (g + 1))
                n = 0
                for late in (0, 1):
                    for c in range(KC):
                        ins = mm(front_ps[0][:, 0:GT], tokw[:, late * KC + c], xT[:, c, :, late:late + S],
                                 start=(n == 0), stop=(n == 2 * KC - 1))
                        n += 1
                ins.then_inc(h_done, 1)

            def centre(g):
                at_least(pe, h_kept, g + 1)
                mm(front_ps[1][:, 0:GT], center[:], hT[:], start=True, stop=True).then_inc(hc_done, 1)

            def variance(g):
                at_least(pe, sq_kept, g + 1)
                mm(front_ps[0][:, 0:GT], average[:], sqA[:], start=True, stop=True).then_inc(var_done, 1)

            def turn_xn(g, q):
                at_least(pe, xnT_kept, g + 1)
                for b in range(GB):
                    ins = nc.tensor.transpose(front_ps[1][0:S, b * D:(b + 1) * D], xnT[:, q, b * S:(b + 1) * S], ident[:])
                ins.then_inc(xn_done, 1)

            def make_z(g, h):
                if h == 0:
                    at_least(pe, xnh_kept, g + 1)
                    at_least(pe, xnl_kept, g + 1)
                if h == 1:
                    at_least(pe, xn_kept, g + 1)
                if h >= 2:
                    at_least(pe, z_kept, H * g + h - 1)
                three(front_ps[h % 2][:, 0:GT], pair_h[:, h], pair_l[:, h], xn_h[:], xn_l[:],
                      True, True).then_inc(z_done, 1)

            for c in range(KC):
                turn_x(0, c, 0, 0)
            embed(0)
            centre(0)
            variance(0)
            turn_xn(0, 0)
            for h in range(H):
                make_z(0, h)

            def step(g, k, i, q):
                more = exists(g + 1)
                if exists(g):
                    n = UN * g + k
                    half, b = k // GB, k % GB
                    at_least(pe, z_kept, H * g + (half + 1) * HH)
                    at_least(pe, cent_kept, n - 1)
                    mm(score_ps[k % 2][0:S, 0:GT], xnT[:, q, b * S:(b + 1) * S], z[:, q, b, half * HH:(half + 1) * HH, :],
                       start=True, stop=True).then_inc(score_done, 1)
                if more:
                    if k == 0:
                        turn_x(g + 1, 0, i + q, 1 - q)
                    if k == 1:
                        embed(g + 1)
                    if k == 2:
                        variance(g + 1)
                    if k == 3:
                        turn_xn(g + 1, 1 - q)
                    if k >= 4:
                        make_z(g + 1, 2 * (k - 4) + 1)
                gv, h = back(g, k, LAG_V)
                if exists(gv):
                    at_least(pe, mix_kept, UN * gv + (h // HH + 1) * GB)
                    at_least(pe, val_kept, H * gv + h)
                    mm(val_ps[:, 0:GT], wvs[:, h], mix[:, h], start=True, stop=True).then_inc(val_done, 1)
                if more:
                    if k == 0:
                        turn_x(g + 1, 1, i + q, 1 - q)
                    if k == 1:
                        centre(g + 1)
                    if 3 <= k < 7:
                        make_z(g + 1, 2 * (k - 3))
                gt, kt = back(g, k, LAG_T)
                if exists(gt):
                    n = UN * gt + kt
                    at_least(pe, prob_kept, n + 1)
                    at_least(pe, probT_kept, n - 1)
                    for m in range(HH):
                        ins = nc.tensor.transpose(probT_ps[kt % 2][0:S, m * S:(m + 1) * S], prob[:, kt % 2, m], ident[0:S, 0:S])
                    ins.then_inc(probT_done, 1)
                gm, km = back(g, k, LAG_M)
                if exists(gm):
                    n = UN * gm + km
                    qm = q if k >= LAG_M else 1 - q
                    at_least(pe, probT_kept, n + 1)
                    at_least(pe, xn_kept, gm + 1)
                    at_least(pe, mix_kept, n)
                    mm(mix_ps[:, 0:GT], xn[:, qm, km % GB], probT[:, km % 2], start=True, stop=True).then_inc(mix_done, 1)

            steps_first(pe, step)

            first_part_over(pe)
            pe.wait_ge(split_lt, 2)
            pe.wait_ge(split_12, 16)
            pe.wait_ge(b2_moved, 48)
            pe.wait_ge(cs, 7 + NE + 4)

            def turn_a(c, j, q):
                m = AC * c + j
                if j == 0:
                    if isinstance(c, int):
                        pe.wait_ge(a_in[q], 32 * (c // 2 + 1))
                    else:
                        pe.wait_ge(a_in[q], 16 * (c - q + 2))
                    at_least(pe, t_kept, c)
                if j == 1:
                    at_least(pe, combT_kept, c)
                at_least(pe, aTl_kept, m - 1)
                for r in range(RT):
                    ins = nc.tensor.transpose(turn_ps[j % 2][:, r * P:(r + 1) * P], arow[:, q, r, j * P:(j + 1) * P], ident[:])
                ins.then_inc(aT_done, 1)

            def project(c, j):
                m = AC * c + j
                if j == 0:
                    at_least(pe, out_kept, c - 1)
                    at_least(pe, h1_kept, c)
                at_least(pe, aTh_kept, m + 1)
                at_least(pe, aTl_kept, m + 1)
                three(proj_ps[:], wlt_h[:, j], wlt_l[:, j], aT_h[:, j % 2], aT_l[:, j % 2],
                      j == 0, j == AC - 1).then_inc(proj_done, 1)

            def centre2(c, q):
                at_least(pe, h1_kept, c + 1)
                at_least(pe, aTl_kept, AC * (c + 1))
                mm(turn_ps[0][:], center[:], h1[:, q], start=True, stop=True).then_inc(hc2_done, 1)

            def variance2(c):
                at_least(pe, sq2_kept, c + 1)
                mm(turn_ps[1][:], average[:], sqB[:], start=True, stop=True).then_inc(var2_done, 1)

            def logits(c):
                at_least(pe, t_kept, c + 1)
                for r in range(RT):
                    o = turn_ps[1][:, r * NE:(r + 1) * NE]
                    mm(o, tT[:, r * P:(r + 1) * P], wrs[:], start=True, stop=False)
                    ins = mm(o, ones_row[:], brs[:], start=False, stop=True)
                ins.then_inc(lg_done, 1)

            def turn_comb(c):
                at_least(pe, comb_kept, 2 * (c + 1))
                for r in range(RT):
                    ins = nc.tensor.transpose(turn_ps[1][0:K3, r * P:(r + 1) * P], comb3[:, r].bitcast(F32), ident[:])
                ins.then_inc(combT_done, 1)

            def turn_out(c, q):
                at_least(pe, acc_kept, NE * (c + 1))
                at_least(pe, h1_kept, c + 1 if isinstance(c, int) and c == NCH - 1 else c + 2)
                for r in range(RT):
                    ins = nc.tensor.transpose(proj_ps[:, r * D:(r + 1) * D], acc[:, q, r * P:(r + 1) * P], ident[:])
                ins.then_inc(outT_done, 1)

            for j in range(AC):
                turn_a(0, j, 0)
                project(0, j)
            centre2(0, 0)
            variance2(0)
            logits(0)
            turn_comb(0)

            def chunk(c, i, q, more):
                for s in range(HS + LAG_Y):
                    if s < HS:
                        n, e, f = HS * c + s, s // FC, s % FC
                        if s == 0:
                            at_least(pe, th_kept, c + 1)
                            at_least(pe, tl_kept, c + 1)
                        at_least(pe, hid_kept, n - 1)
                        three(hid_ps[s % 2][:], w1_h[:, e, f * P:(f + 1) * P], w1_l[:, e, f * P:(f + 1) * P],
                              t_h[:, q], t_l[:, q], True, True).then_inc(hid_done, 1)
                    if s == 0:
                        at_least(pe, combT_kept, c + 1)
                        at_least(pe, gate_kept, NE * c)
                        mm(gate_ps[:], b2_3[:], combT[:, q], start=True, stop=True).then_inc(bias_done, 1)
                    if s < HS and s % FC == 1:
                        m = NE * c + e
                        if e == 0:
                            at_least(pe, acc_begun, c + 1)
                        else:
                            at_least(pe, gate_kept, m)
                        mm(gate_ps[:], pick[:, e], combT[:, q], start=True, stop=True).then_inc(gate_done, 1)
                    if s == 2 and (not isinstance(c, int) or c > 0):
                        turn_out(c - 1, 1 - q)
                    if more:
                        if s % 2 == 0 and s < 2 * AC:
                            turn_a(c + 1, s // 2, 1 - q)
                        if s % 2 == 1 and 3 <= s < 2 * AC + 2:
                            project(c + 1, (s - 3) // 2)
                        if s == 19:
                            centre2(c + 1, 1 - q)
                        if s == 21:
                            variance2(c + 1)
                        if s == 25:
                            logits(c + 1)
                        if s == 30:
                            turn_comb(c + 1)
                    if s >= LAG_Y:
                        y = s - LAG_Y
                        ye, yf = y // FC, y % FC
                        n = HS * c + y
                        at_least(pe, hidh_kept, n + 1)
                        at_least(pe, hidl_kept, n + 1)
                        if yf == 0:
                            at_least(pe, gated_kept, NE * c + ye - 1)
                        three(y_ps[ye % 2][:], w2_h[:, y], w2_l[:, y], hid_h[:, y % 4], hid_l[:, y % 4],
                              yf == 0, yf == FC - 1).then_inc(used, 1)

            steps_second(pe, chunk)
            turn_out(NCH - 1, (NCH - 1) % 2)


_INS = ['x', 'L0_tok_W', 'L0_tok_b', 'L0_attn_Wq', 'L0_attn_Wk', 'L0_attn_Wv', 'L0_attn_Wlt', 'L0_ffn_Wr',
        'L0_ffn_br', 'L0_ffn_W1', 'L0_ffn_b1', 'L0_ffn_W2', 'L0_ffn_b2']


def kernel(**inputs):
    import numpy as _np
    import concourse.bacc as _bacc
    from concourse import mybir as _mybir
    from concourse.bass_utils import run_bass_kernel_spmd as _run

    nc = _bacc.Bacc("TRN2", target_bir_lowering=False, num_devices=1)
    arrays, args = {}, []
    for name in _INS:
        a = _np.ascontiguousarray(inputs[name])
        arrays[f"in_{name}_dram"] = a
        args.append(nc.dram_tensor(f"in_{name}_dram", a.shape, _mybir.dt.from_np(a.dtype), kind="ExternalInput").ap())
    args.append(nc.dram_tensor("out_0_dram", (T, D), F32, kind="ExternalOutput").ap())
    build(nc, *args)
    r = _run(nc, [arrays], core_ids=[0])
    return r.results[0]["out_0_dram"].reshape(B, S, D)
```

```python
from contextlib import ExitStack

import concourse.bass as bass
from concourse import mybir

ALU = mybir.AluOpType
ACT = mybir.ActivationFunctionType
F32 = mybir.dt.float32
F32R = mybir.dt.float32r
I32 = mybir.dt.int32
AX_X = mybir.AxisListType.X

P = 128
B, L, FEAT = 128, 750, 32
PATCH, STRIDE = 16, 8
S = (L - PATCH) // STRIDE + 1
D = 128
H, E = 8, 64
NE, FF = 8, 512
FC = FF // P
EPS = 1e-5
T = B * S
ROW = STRIDE * FEAT
NROW = S + 1
KC = ROW // P

GB = 4
NG = B // GB
GT = GB * S
HH = H // 2
UN = 2 * GB
LAG_S, LAG_T, LAG_TK, LAG_M, LAG_V = 1, 2, 3, 4, 8

CT = 512
NCH = T // CT
RT = CT // P
NT = T // P
AC = H * D // P

ROWW = D + 4
ROOM = T + P
TILES = 2 * NT + NE
SPARE = TILES - 2 * NT
SORTED_ROWS = NE * ROOM + SPARE * P
Y_ROWS = 2 * T + (NE + SPARE) * P
RING = 8
LAG_H, LAG_R, LAG_Y = 1, 2, 3
SETUP = 8
FIN = 4
assert TILES % RING == 0 and T % CT == 0 and GT <= 512 and HH * S == GT and H * S * D == S * H * D


def at_least(eng, sem, value):
    if isinstance(value, int) and value <= 0:
        return
    eng.wait_ge(sem, value)


def back(g, k, lag):
    k -= lag
    while k < 0:
        g, k = g - 1, k + UN
    return g, k


def exists(g):
    return not isinstance(g, int) or 0 <= g < NG


def build(nc, x, tok_w, tok_b, wq, wk, wv, wlt, wr, br, w1, b1, w2, b2, out):
    ax_dram = nc.dram_tensor("ax_scratch", (T * H * D,), F32, kind="Internal").ap()
    h_dram = nc.dram_tensor("h_scratch", (D, T), F32, kind="Internal").ap()
    sorted_dram = nc.dram_tensor("sorted_scratch", (SORTED_ROWS, ROWW), F32, kind="Internal").ap()
    y_dram = nc.dram_tensor("y_scratch", (Y_ROWS, D), F32, kind="Internal").ap()
    ax_in = ax_dram.rearrange("(b f h i) -> b f h i", f=D, h=H, i=S)
    ax_rows = ax_dram.rearrange("(t c) -> t c", c=H * D)
    x_rows = x.rearrange("b l f -> b (l f)")

    with ExitStack() as ctx, nc.allow_non_contiguous_dma("biases once"):
        def sb(name, shape, dt=F32, stack=ctx):
            return stack.enter_context(nc.sbuf_tensor(name, shape, dt))

        def sem(name):
            return ctx.enter_context(nc.semaphore(name))

        ident = sb("ident", [P, P])
        center = sb("center", [P, P])
        average = sb("average", [P, P])
        ones = sb("ones", [P, P])
        before = sb("before", [P, P])
        wlt_h = sb("wlt_h", [P, AC, D], F32R)
        wlt_l = sb("wlt_l", [P, AC, D], F32R)
        w1_h = sb("w1_h", [D, NE * FF], F32R)
        w1_l = sb("w1_l", [D, NE * FF], F32R)
        loading = ExitStack()
        w2raw = sb("w2raw", [P, NE * FC, 2, D], stack=loading)
        loading.close()
        w2s = sb("w2s", [P, NE * FC, 2, D], F32R)
        wrs = sb("wrs", [D, NE])
        brs = sb("brs", [P, NE])
        before_r = sb("before_r", [P, P], F32R)
        ones_r = sb("ones_r", [P, P], F32R)
        power = sb("power", [P, GB])
        ones2 = sb("ones2", [2, P], F32R)
        b2s = sb("b2s", [2, NE * D], F32R)
        rank = sb("rank", [P, RT, NE])

        arow0 = sb("arow0", [P, RT, H * D])
        raw = arow0[:].rearrange("p r n -> p (r n)")
        hch0 = sb("hch0", [D, CT])

        first = ExitStack()
        tokw = sb("tokw", [P, 2 * KC, D], stack=first)
        tokb = sb("tokb", [D, 1], stack=first)
        pair_h = sb("pair_h", [D, H, D], F32R, stack=first)
        pair_l = sb("pair_l", [D, H, D], F32R, stack=first)
        wv_h = sb("wv_h", [D, H, D], F32R, stack=first)
        wv_l = sb("wv_l", [D, H, D], F32R, stack=first)
        b2raw = sb("b2raw", [1, NE * D], stack=first)
        b2_l = sb("b2_l", [1, NE * D], F32R, stack=first)
        xin = sb("xin", [NROW, 2, GB, ROW], stack=first)
        xT = sb("xT", [P, KC, GB, NROW], stack=first)
        hT = sb("hT", [D, GT], stack=first)
        sqA = sb("sqA", [D, GT], stack=first)
        hcA = sb("hcA", [D, GT], stack=first)
        varA = sb("varA", [S, GB], stack=first)
        rstdA = sb("rstdA", [S, GB], stack=first)
        diag = sb("diag", [S, GB, S], stack=first)
        xnT = sb("xnT", [D, 2, GT], stack=first)
        xn_h = sb("xn_h", [D, GT], F32R, stack=first)
        xn_l = sb("xn_l", [D, GT], F32R, stack=first)
        xtok_h = sb("xtok_h", [S, 2, GB, D], F32R, stack=first)
        xtok_l = sb("xtok_l", [S, 2, GB, D], F32R, stack=first)
        z = sb("z", [D, 2, GB, H, S], stack=first)
        peak = sb("peak", [S, 2, HH], stack=first)
        cent = sb("cent", [S, 2, HH, S], stack=first)
        expo = sb("expo", [S, 2, HH, S], stack=first)
        total = sb("total", [S, 2, HH], stack=first)
        inv = sb("inv", [S, 2, HH], stack=first)
        prob = sb("prob", [S, 2, HH, S], stack=first)
        probT_h = sb("probT_h", [S, 2, HH, S], F32R, stack=first)
        probT_l = sb("probT_l", [S, 2, HH, S], F32R, stack=first)
        mix_room = w2s[:].rearrange("p a h d -> p (a h d)")
        mix_h, mix_l = (mix_room[:, j * H * GT:(j + 1) * H * GT].rearrange("d (h b i) -> d h b i", h=H, b=GB)
                        for j in (0, 1))
        val = sb("val", [D, 2, GB, HH, S], stack=first)
        wv_raw = val[:].rearrange("d a b h i -> d (a b h i)")[:, 0:H * D].rearrange("d (h f) -> d h f", h=H)
        first.close()

        h1tok = sb("h1tok", [P, NT, D])
        wtab = sb("wtab", [P, 2, NT])

        padi = sb("padi", [1, NE], I32)
        whosei = sb("whosei", [1, TILES + 12], I32)
        wherei = sb("wherei", [1, TILES], I32)
        goals = sb("goals", [P, RING], I32)

        second = ExitStack()
        arow = [arow0, sb("arow1", [P, RT, H * D], stack=second)]
        hch = [hch0, sb("hch1", [D, CT], stack=second)]
        aT_h = sb("aT_h", [P, 2, CT], F32R, stack=second)
        aT_l = sb("aT_l", [P, 2, CT], F32R, stack=second)
        h1 = sb("h1", [D, 2, CT], stack=second)
        sqB = sb("sqB", [D, CT], stack=second)
        hcB = sb("hcB", [D, CT], stack=second)
        varB = sb("varB", [P, RT], stack=second)
        rstdB = sb("rstdB", [P, 2, RT], stack=second)
        lg = sb("lg", [P, RT, NE], stack=second)
        eq = sb("eq", [P, RT, NE], stack=second)
        key = sb("key", [P, RT, NE], stack=second)
        one1 = sb("one1", [P, RT, NE], stack=second)
        one2 = sb("one2", [P, RT, NE], stack=second)
        mask = sb("mask", [P, RT, NE], F32R, stack=second)
        place = sb("place", [P, RT, NE], stack=second)
        top = sb("top", [P, 8, RT], stack=second)
        base = sb("base", [P, NE], stack=second)
        posf = sb("posf", [P, 2, RT], stack=second)
        posi = sb("posi", [P, 2, 2, RT], I32, stack=second)
        goal = sb("goal", [P, 2, RT], stack=second)
        trow = sb("trow", [P, 2, 2, RT, ROWW], stack=second)
        blank = sb("blank", [P, NE + SPARE, ROWW], stack=second)
        ebase = sb("ebase", [P, NE], stack=second)
        held = sb("held", [1, NE], stack=second)
        bound = sb("bound", [1, NE, NT], stack=second)
        ntile = sb("ntile", [1, NE], stack=second)
        jump = sb("jump", [1, NE], stack=second)
        cum = sb("cum", [1, NE + 1], stack=second)
        tile_no = sb("tile_no", [1, TILES], stack=second)
        past = sb("past", [1, TILES], stack=second)
        whose = sb("whose", [1, TILES], stack=second)
        where = sb("where", [1, TILES], stack=second)
        second.close()

        third = ExitStack()
        b1b = sb("b1b", [P, NE * FF], stack=third)
        tin = sb("tin", [P, RING, ROWW], stack=third)
        x_h = sb("x_h", [D, 2, P], F32R, stack=third)
        x_l = sb("x_l", [D, 2, P], F32R, stack=third)
        pre = sb("pre", [P, 2, FF], stack=third)
        hid_h = sb("hid_h", [P, 2, FF], F32R, stack=third)
        hid_l = sb("hid_l", [P, 2, FF], F32R, stack=third)
        ytok = sb("ytok", [P, 4, D], stack=third)
        yin = sb("yin", [P, FIN, 2, RT, D], stack=third)
        osb = sb("osb", [P, FIN, RT, D], stack=third)
        third.close()

        bank = [ctx.enter_context(nc.psum_tensor(f"bank{i}", [P, 512], F32)) for i in range(8)]
        front_ps, score_ps, probT_ps, mix_ps, val_ps = bank[0:2], bank[2:4], bank[4:6], bank[6], bank[7]
        turn_ps, proj_ps, tok_ps, res_ps, count_ps, hc_ps, var_ps = bank[0:2], bank[2], bank[3], bank[4], bank[5], bank[6], bank[7]
        xt_ps, hid_ps, back_ps, y_ps = bank[0], bank[1:3], bank[3:5], bank[5:7]

        ws_small, ws_tok, ws_qk, ws_v, ws_lt, ws_1, ws_2 = (sem(n) for n in (
            "ws_small", "ws_tok", "ws_qk", "ws_v", "ws_lt", "ws_1", "ws_2"))
        cs = sem("cs")
        qkT_done, qkT_kept, pair_done, pair_kept = (sem(n) for n in ("qkT_done", "qkT_kept", "pair_done", "pair_kept"))
        split_lt, split_12, split_b2, b2_moved = (sem(n) for n in ("split_lt", "split_12", "split_b2", "b2_moved"))
        x_in = [sem("x_in0"), sem("x_in1")]
        xT_done, xT_kept, h_done, h_kept, h_out = (sem(n) for n in ("xT_done", "xT_kept", "h_done", "h_kept", "h_out"))
        hc_done, sq_kept, hcs_kept, var_done, var_kept, rstd_kept, diag_kept, spread_done = (sem(n) for n in (
            "hc_done", "sq_kept", "hcs_kept", "var_done", "var_kept", "rstd_kept", "diag_kept", "spread_done"))
        xnT_kept, xnh_kept, xnl_kept, xn_done, xtokh_kept, xtokl_kept = (sem(n) for n in (
            "xnT_kept", "xnh_kept", "xnl_kept", "xn_done", "xtokh_kept", "xtokl_kept"))
        z_done, z_kept = sem("z_done"), sem("z_kept")
        score_done, peak_kept, cent_kept, exp_kept, total_kept, inv_kept = (sem(n) for n in (
            "score_done", "peak_kept", "cent_kept", "exp_kept", "total_kept", "inv_kept"))
        prob_kept, probT_done, probTh_kept, probTl_kept = (sem(n) for n in (
            "prob_kept", "probT_done", "probTh_kept", "probTl_kept"))
        mix_done, mixh_kept, mixl_kept, val_done, val_kept = (sem(n) for n in (
            "mix_done", "mixh_kept", "mixl_kept", "val_done", "val_kept"))
        val_out = [sem("val_out0"), sem("val_out1")]
        a_in = [sem("a_in0"), sem("a_in1")]
        aT_done, aTh_kept, aTl_kept, proj_done, h1_kept = (sem(n) for n in (
            "aT_done", "aTh_kept", "aTl_kept", "proj_done", "h1_kept"))
        hc2_done, sq2_kept, hcs2_kept, var2_done, var2_kept, rstd2_kept = (sem(n) for n in (
            "hc2_done", "sq2_kept", "hcs2_kept", "var2_done", "var2_kept", "rstd2_kept"))
        lg_done, route, mask_kept, gap_kept, gapexp_kept, count_done, posi_kept = (sem(n) for n in (
            "lg_done", "route", "mask_kept", "gap_kept", "gapexp_kept", "count_done", "posi_kept"))
        tok_done, trow1_kept, trow2_kept, res_done, res_kept, goal_kept = (sem(n) for n in (
            "tok_done", "trow1_kept", "trow2_kept", "res_done", "res_kept", "goal_kept"))
        scattered = [sem("scattered0"), sem("scattered1")]
        passed = sem("passed")
        table, pads_in, b1_in = sem("table"), sem("pads_in"), sem("b1_in")
        tile_in = [sem(f"tile_in{i}") for i in range(RING)]
        xt_done, xh_kept, xl_kept, goal_read = (sem(n) for n in ("xt_done", "xh_kept", "xl_kept", "goal_read"))
        hid_done, pre_kept, back_done, hidh_kept, hidl_kept, y_done, y_kept = (sem(n) for n in (
            "hid_done", "pre_kept", "back_done", "hidh_kept", "hidl_kept", "y_done", "y_kept"))
        y_out = [sem(f"y_out{i}") for i in range(4)]
        y_in = [sem(f"y_in{i}") for i in range(FIN)]
        sum1_kept, sum2_kept = sem("sum1_kept"), sem("sum2_kept")
        out_sent = [sem(f"out_sent{i}") for i in range(FIN)]

        Z_FIRST = {5: (1,), 6: (3,), 7: (6,)}
        Z_THEN = {4: (0,), 5: (2,), 6: (4, 5), 7: (7,)}

        block = ctx.enter_context(nc.Block())
        mm = nc.tensor.matmul

        def three(dst, wh, wl, vh, vl, start, stop):
            mm(dst, wh, vh, start=start, stop=False)
            mm(dst, wh, vl, start=False, stop=False)
            return mm(dst, wl, vh, start=False, stop=stop)

        def steps_first(eng, step):
            for g in (0, 1):
                for k in range(UN):
                    step(g, k, 0, g)
            with eng.Fori(1, NG // 2 - 1) as i:
                for q in (0, 1):
                    for k in range(UN):
                        step(2 * i + q, k, i, q)
            for g in (NG - 2, NG - 1):
                for k in range(UN):
                    step(g, k, NG // 2 - 1, g % 2)
            for k in range(LAG_V):
                step(NG, k, NG // 2, 0)

        def steps_second(eng, chunk):
            chunk(0, 0, 0, True)
            chunk(1, 0, 1, True)
            chunk(2, 1, 0, True)
            with eng.Fori(1, (NCH - 3) // 2) as i:
                chunk(2 * i + 1, i, 1, True)
                chunk(2 * i + 2, i + 1, 0, True)
            chunk(NCH - 2, (NCH - 3) // 2, 1, True)
            chunk(NCH - 1, (NCH - 1) // 2, 0, False)

        def blocks(eng, total, size, step):
            for n in range(size):
                step(n, 0, n)
            with eng.Fori(1, total // size) as i:
                for q in range(size):
                    step(size * i + q, i, q)
            for n in range(total // size * size, total):
                step(n, n // size, n % size)

        def tiles(eng, step):
            blocks(eng, TILES, RING, step)
            for n in range(TILES, TILES + LAG_Y + 1):
                step(n, n // RING, n % RING)

        def tile_experts(eng, i):
            sl = slice(RING * i, RING * i + 12) if isinstance(i, int) else bass.ds(RING * i, 12)
            regs = expert_regs[eng.engine]
            eng.load(regs, whosei[0:1, sl])
            return [eng.snap(r, min_val=0, max_val=NE - 1) for r in regs]

        expert_regs = {eng.engine: [eng.alloc_register(f"expert{j}") for j in range(12)] for eng in (nc.tensor, nc.vector)}

        def is_tile(n):
            return not isinstance(n, int) or 0 <= n < TILES

        def pool_waits(*waits):
            for sm, v in waits:
                at_least(nc.gpsimd, sm, v)
            nc.gpsimd.sem_inc(passed, 1)

        def first_part_over(eng):
            eng.wait_ge(h_out, 16 * NG)
            for half in (0, 1):
                eng.wait_ge(val_out[half], 16 * NG)

        @block.sync
        def _(sp):
            sp.dma_start(tokw[:], tok_w.rearrange("(c p) d -> p c d", p=P)).then_inc(ws_tok, 16)
            sp.dma_start(raw[:, 0:H * E], wq.rearrange("h d e -> d h e")).then_inc(ws_qk, 16)
            sp.dma_start(raw[:, H * E:2 * H * E], wk.rearrange("h d e -> d h e")).then_inc(ws_qk, 16)
            sp.dma_start(wv_raw, wv.rearrange("h d f -> d h f")).then_inc(ws_v, 16)

            def load_x(g, i, q):
                at_least(sp, xT_done, KC * (g - 1))
                if isinstance(g, int):
                    src = x_rows[g * GB:(g + 1) * GB, 0:NROW * ROW]
                else:
                    src = x_rows[bass.ds(g * GB, GB), 0:NROW * ROW]
                sp.dma_start(xin[:, q], src.rearrange("b (r c) -> r b c", c=ROW)).then_inc(x_in[q], 16)

            def store_h(g):
                at_least(sp, h_kept, g + 1)
                dst = h_dram[:, g * GT:(g + 1) * GT] if isinstance(g, int) else h_dram[:, bass.ds(g * GT, GT)]
                sp.dma_start(dst, hT[:]).then_inc(h_out, 16)

            load_x(0, 0, 0)
            load_x(1, 0, 1)
            store_h(0)

            def step(g, k, i, q):
                nxt = g + 1
                if k == 2 and exists(g + 2):
                    load_x(g + 2, i + 1, q)
                if k == 3 and exists(nxt):
                    store_h(nxt)
                gv, h = back(g, k, LAG_V)
                if h % HH == HH - 1 and exists(gv):
                    half = h // HH
                    at_least(sp, val_kept, H * gv + h + 1)
                    dst = ax_in[gv * GB:(gv + 1) * GB] if isinstance(gv, int) else ax_in[bass.ds(gv * GB, GB)]
                    sp.dma_start(dst[:, :, half * HH:(half + 1) * HH, :].rearrange("b f h i -> f b (h i)"),
                                 val[:, half].rearrange("f b h i -> f b (h i)")).then_inc(val_out[half], 16)

            steps_first(sp, step)

            def load_a(c, i, q):
                at_least(sp, aT_done, AC * (c - 1))
                at_least(sp, h1_kept, c - 1)
                if isinstance(c, int):
                    rows, cols = ax_rows[c * CT:(c + 1) * CT, :], h_dram[:, c * CT:(c + 1) * CT]
                else:
                    rows, cols = ax_rows[bass.ds(c * CT, CT), :], h_dram[:, bass.ds(c * CT, CT)]
                sp.dma_start(arow[q][:], rows.rearrange("(r p) n -> p r n", p=P)).then_inc(a_in[q], 16)
                sp.dma_start(hch[q][:], cols).then_inc(a_in[q], 16)

            sp.wait_ge(split_12, 8)
            for half in (0, 1):
                sp.wait_ge(val_out[half], 16 * (CT // GT + 1))
            load_a(0, 0, 0)
            first_part_over(sp)
            load_a(1, 0, 1)

            def chunk(c, i, q, more):
                if not isinstance(c, int) or c + 2 < NCH:
                    load_a(c + 2, i + 1, q)

            steps_second(sp, chunk)

            sp.wait_ge(table, 1)
            sp.dma_start(b1b[:], b1.rearrange("e f -> (e f)").partition_broadcast(P)).then_inc(b1_in, 16)
            sp.wait_ge(pads_in, 16 * (NE + SPARE))
            for half in (0, 1):
                sp.wait_ge(scattered[half], 16 * 2 * RT * ((NCH + 1 - half) // 2))

            def load_tile(n, i, q):
                at_least(sp, xt_done, n - RING + 1)
                at_least(sp, goal_read, n - RING + 1)
                row = sp.value_load(wherei[0:1, bass.ds(n, 1)], min_val=0, max_val=SORTED_ROWS - P)
                sp.dma_start(tin[:, q], sorted_dram[bass.ds(row, P), :]).then_inc(tile_in[q], 16)

            blocks(sp, TILES, RING, load_tile)

            for j in range(4):
                sp.wait_ge(y_out[j], 16 * (TILES // 4))

            def rows(ap, c, first):
                sl = slice(first + c * CT, first + (c + 1) * CT) if isinstance(c, int) else bass.ds(c * CT + first, CT)
                return ap[sl, :].rearrange("(r p) d -> p r d", p=P)

            def load_y(c, i, q):
                at_least(sp, sum2_kept, c - FIN + 1)
                for choice in (0, 1):
                    sp.dma_start(yin[:, q, choice], rows(y_dram, c, (1 - choice) * T)).then_inc(y_in[q], 16)

            blocks(sp, NCH, FIN, load_y)
            sp.wait_ge(sum2_kept, NCH)

        @block.gpsimd
        def _(pool):
            count = [0]

            def const(ins):
                count[0] += 1
                ins.then_inc(cs, 1)
                return count[0]

            const(pool.memset(ident[:], 0.0))
            const(pool.memset(average[:], 1.0 / D))
            const(pool.memset(center[:], -1.0 / D))
            const(pool.memset(power[:], -0.5))
            const(pool.memset(ones[:], 1.0))
            const(pool.memset(before[:], 1.0))
            pool.wait_ge(cs, count[0])
            const(pool.affine_select(out=ident[:], in_=ident[:], compare_op=ALU.not_equal, fill=1.0, base=0,
                                     pattern=[[-1, P]], channel_multiplier=1))
            const(pool.affine_select(out=center[:], in_=center[:], compare_op=ALU.not_equal, fill=1.0 - 1.0 / D,
                                     base=0, pattern=[[-1, P]], channel_multiplier=1))
            const(pool.affine_select(out=before[:], in_=before[:], compare_op=ALU.is_gt, fill=0.0, base=0,
                                     pattern=[[1, P]], channel_multiplier=-1))
            assert count[0] == 9
            for e in range(NE):
                const(pool.memset(rank[:, :, e:e + 1], float(NE - e)))

            def split(src, high, low, n):
                pool.tensor_copy(high, src).then_inc(split_12, 1)
                pool.wait_ge(split_12, n)
                pool.tensor_tensor(low, src, high.bitcast(F32), ALU.subtract).then_inc(split_12, 1)

            def scale_prob(g, k):
                n = UN * g + k
                at_least(pool, inv_kept, n + 1)
                at_least(pool, exp_kept, n + 1)
                at_least(pool, probT_done, n - 1)
                nc.gpsimd.tensor_tensor(prob[:, k % 2], expo[:, k % 2],
                                        inv[:, k % 2].unsqueeze(2).to_broadcast([S, HH, S]), ALU.mult).then_inc(prob_kept, 1)

            def root(g):
                at_least(pool, var_kept, g + 1)
                at_least(pool, diag_kept, g)
                nc.gpsimd.tensor_tensor(rstdA[:], varA[:], power[0:S, :], ALU.pow).then_inc(rstd_kept, 1)

            def low_xn(g, q):
                at_least(pool, xnh_kept, g + 1)
                at_least(pool, z_done, H * g)
                nc.gpsimd.tensor_tensor(xn_l[:], xnT[:, q], xn_h[:].bitcast(F32), ALU.subtract).then_inc(xnl_kept, 1)

            root(0)
            low_xn(0, 0)
            pool.wait_ge(pair_kept, 1)
            pool.wait_ge(split_lt, 2)
            pool.dma_start(raw, w1.rearrange("e d f -> d e f")).then_inc(ws_1, 16)

            def step(g, k, i, q):
                if k == 2 and exists(g + 1):
                    root(g + 1)
                if k == 3 and exists(g + 1):
                    low_xn(g + 1, 1 - q)
                if exists(g):
                    scale_prob(g, k)
                if isinstance(g, int) and g == 0 and k in (1, 3, 5, 7):
                    j = (k - 1) // 2
                    sl = slice(j * 1024, (j + 1) * 1024)
                    if k == 1:
                        pool.wait_ge(ws_1, 16)
                    split(raw[:, sl], w1_h[:, sl], w1_l[:, sl], 2 * j + 1)

            steps_first(pool, step)

            first_part_over(pool)
            pool.dma_start(w2raw[:, :, 1], w2.rearrange("e (c p) d -> p (e c) d", p=P)).then_inc(ws_2, 16)
            laid = [0]

            def lay(ins):
                laid[0] += 1
                ins.then_inc(goal_kept, 1)
                pool.wait_ge(goal_kept, laid[0])

            lay(pool.iota(base[:], pattern=[[ROOM, NE]], base=0, channel_multiplier=0,
                          allow_small_or_imprecise_dtypes=True))
            lay(pool.iota(ebase[:], pattern=[[ROOM, NE]], base=0, channel_multiplier=0,
                          allow_small_or_imprecise_dtypes=True))
            lay(pool.iota(goal[:], pattern=[[-T, 2], [P, RT]], base=T, channel_multiplier=1,
                          allow_small_or_imprecise_dtypes=True))
            lay(pool.iota(bound[:], pattern=[[0, NE], [P, NT]], base=0, channel_multiplier=0,
                          allow_small_or_imprecise_dtypes=True))
            lay(pool.iota(tile_no[:], pattern=[[1, TILES]], base=0, channel_multiplier=0,
                          allow_small_or_imprecise_dtypes=True))
            lay(pool.memset(trow[:, :, :, :, D:ROWW], 0.0))
            lay(pool.memset(blank[:], 0.0))
            lay(pool.iota(blank[:, :, D:D + 1].bitcast(I32), pattern=[[P, NE + SPARE]], base=2 * T, channel_multiplier=1))
            LAID = laid[0]
            assert LAID == SETUP
            for k in range(SPARE):
                row = NE * ROOM + k * P
                pool.dma_start(sorted_dram[row:row + P, :], blank[:, NE + k]).then_inc(pads_in, 16)

            def root2(c, q):
                at_least(pool, var2_kept, c + 1)
                at_least(pool, trow1_kept, c - 1)
                nc.gpsimd.tensor_tensor(rstdB[:, q], varB[:], power[:], ALU.pow).then_inc(rstd2_kept, 1)

            def set_goals(c, q):
                pool_waits((scattered[q], 16 * 2 * RT * (c // 2) if isinstance(c, int) else 8 * 2 * RT * (c - q)))
                nc.gpsimd.tensor_copy(trow[:, q, :, :, D:D + 1].bitcast(I32), goal[:].unsqueeze(3)).then_inc(goal_kept, 1)
                pool_waits((goal_kept, LAID + 2 * c + 1))
                nc.gpsimd.tensor_scalar(goal[:], goal[:], float(CT), None, ALU.add).then_inc(goal_kept, 1)

            def scatter(c, q, choice):
                if choice == 0:
                    pool_waits((goal_kept, LAID + 2 * c + 2), (trow1_kept, c + 1), (posi_kept, c + 1))
                else:
                    pool_waits((trow2_kept, c + 1))
                for r in range(RT):
                    pool.indirect_dma_start(
                        out=sorted_dram, out_offset=bass.IndirectOffsetOnAxis(ap=posi[:, q, choice, r:r + 1], axis=0),
                        in_=trow[:, q, choice, r], in_offset=None).then_inc(scattered[q], 16)

            def chunk(c, i, q, more):
                after_first = not isinstance(c, int) or c > 0
                root2(c, q)
                if after_first:
                    for choice in (0, 1):
                        scatter(c - 1, 1 - q, choice)
                set_goals(c, q)
                if isinstance(c, int) and c in (1, 2):
                    if c == 1:
                        pool.wait_ge(ws_2, 16)
                    for j in (2 * c - 2, 2 * c - 1):
                        a = slice(8 * j, 8 * j + 8)
                        split(w2raw[:, a, 1], w2s[:, a, 0], w2s[:, a, 1], 8 + 2 * j + 1)

            steps_second(pool, chunk)
            for choice in (0, 1):
                scatter(NCH - 1, (NCH - 1) % 2, choice)
            pool.wait_ge(table, 1)
            for half in (0, 1):
                pool.wait_ge(scattered[half], 16 * 2 * RT * ((NCH + 1 - half) // 2))
            for e in range(NE):
                row = pool.value_load(padi[0:1, e:e + 1], min_val=e * ROOM, max_val=e * ROOM + T)
                pool.dma_start(sorted_dram[bass.ds(row, P), :], blank[:, e]).then_inc(pads_in, 16)
            pool.wait_ge(pads_in, 16 * (NE + SPARE))

            def tile(n, i, q):
                if is_tile(n):
                    pool_waits((tile_in[q], 16 * (i + 1)),
                               (y_out[q % 4], 16 * (2 * (i - 1) + q // 4 + 1)))
                    nc.gpsimd.tensor_copy(goals[:, q:q + 1], tin[:, q, D:D + 1].bitcast(I32)).then_inc(goal_read, 1)
                m = n - LAG_Y - 1
                if is_tile(m):
                    qm = (q - LAG_Y - 1) % RING
                    pool_waits((goal_read, m + 1),
                               (y_kept, m + 1))
                    pool.indirect_dma_start(out=y_dram, out_offset=bass.IndirectOffsetOnAxis(ap=goals[:, qm:qm + 1], axis=0),
                                            in_=ytok[:, qm % 4], in_offset=None).then_inc(y_out[qm % 4], 16)

            tiles(pool, tile)

        @block.scalar
        def _(act):
            A = nc.scalar.activation
            act.dma_start(tokb[:], tok_b.rearrange("(d o) -> d o", o=1)).then_inc(ws_small, 16)
            act.dma_start(wrs[:], wr).then_inc(ws_small, 16)
            act.dma_start(brs[:], br.partition_broadcast(P)).then_inc(ws_small, 16)
            act.dma_start(b2raw[:], b2.rearrange("(o e) d -> o (e d)", o=1)).then_inc(ws_small, 16)
            act.dma_start(raw[:, 2 * H * E:2 * H * E + AC * D], wlt.rearrange("(c p) d -> p c d", p=P)).then_inc(ws_lt, 16)
            act.wait_ge(ws_small, 4 * 16)
            act.wait_ge(cs, 9)

            def keep_xT(g, c):
                at_least(act, xT_done, KC * g + c + 1)
                at_least(act, h_done, g)
                A(xT[:, c], front_ps[c][:, 0:GB * NROW].rearrange("p (b r) -> p b r", b=GB), ACT.Copy).then_inc(xT_kept, 1)

            def keep_h(g):
                at_least(act, h_done, g + 1)
                at_least(act, hc_done, g)
                at_least(act, h_out, 16 * g)
                A(hT[:], front_ps[0][:, 0:GT], ACT.Identity, bias=tokb[:]).then_inc(h_kept, 1)

            def keep_sq(g):
                at_least(act, hc_done, g + 1)
                at_least(act, var_done, g)
                A(sqA[:], front_ps[1][:, 0:GT], ACT.Square).then_inc(sq_kept, 1)

            def keep_hc(g):
                at_least(act, xnT_kept, g)
                A(hcA[:], front_ps[1][:, 0:GT], ACT.Copy).then_inc(hcs_kept, 1)

            def keep_xnh(g, q):
                at_least(act, xnT_kept, g + 1)
                at_least(act, z_done, H * g)
                at_least(act, xnl_kept, g)
                A(xn_h[:], xnT[:, q], ACT.Copy).then_inc(xnh_kept, 1)

            def keep_xtokh(g, q):
                at_least(act, xn_done, g + 1)
                at_least(act, mix_done, UN * (g - 1))
                A(xtok_h[:, q], front_ps[1][0:S, :].rearrange("t (b d) -> t b d", b=GB), ACT.Copy).then_inc(xtokh_kept, 1)

            def keep_z(g, h, q):
                at_least(act, z_done, H * g + h + 1)
                at_least(act, score_done, UN * (g - 1))
                A(z[:, q, :, h, :], front_ps[h % 2][:, 0:GT].rearrange("d (b j) -> d b j", b=GB),
                  ACT.Copy).then_inc(z_kept, 1)

            for c in range(KC):
                keep_xT(0, c)
            keep_h(0)
            keep_sq(0)
            keep_hc(0)
            keep_xnh(0, 0)
            keep_xtokh(0, 0)
            for h in range(H):
                keep_z(0, h, 0)
            act.wait_ge(split_b2, 2)
            act.dma_start(b2s[1:2, :].bitcast(F32), b2_l[:].bitcast(F32)).then_inc(b2_moved, 16)

            def step(g, k, i, q):
                more = exists(g + 1)
                gt, kt = back(g, k, LAG_TK)
                if exists(gt):
                    n = UN * gt + kt
                    at_least(act, probT_done, n + 1)
                    at_least(act, mix_done, n - 1)
                    A(probT_h[:, kt % 2], probT_ps[kt % 2][0:S, 0:GT].rearrange("j (h i) -> j h i", h=HH),
                      ACT.Copy).then_inc(probTh_kept, 1)
                if more:
                    if k == 0:
                        keep_xT(g + 1, 0)
                    if k == 4:
                        keep_xtokh(g + 1, 1 - q)
                    for h in Z_FIRST.get(k, ()):
                        keep_z(g + 1, h, 1 - q)
                if exists(g):
                    n = UN * g + k
                    at_least(act, cent_kept, n + 1)
                    at_least(act, prob_kept, n - 1)
                    A(expo[:, k % 2], cent[:, k % 2], ACT.Exp, scale=1.0 / E).then_inc(exp_kept, 1)
                if more:
                    if k == 0:
                        keep_xT(g + 1, 1)
                    if k == 1:
                        keep_h(g + 1)
                gm, km = back(g, k, LAG_M)
                if exists(gm):
                    n = UN * gm + km
                    half, b = km // GB, km % GB
                    at_least(act, mix_done, n + 1)
                    at_least(act, val_done, H * gm + HH * half - HH)
                    A(mix_h[:, half * HH:(half + 1) * HH, b, :],
                      mix_ps[:, 0:GT].rearrange("d (h i) -> d h i", h=HH), ACT.Copy).then_inc(mixh_kept, 1)
                gv, h = back(g, k, LAG_V)
                if exists(gv):
                    a = H * gv + h
                    half = h // HH
                    at_least(act, val_done, a + 1)
                    if h % HH == 0:
                        at_least(act, val_out[half], 16 * gv)
                    A(val[:, half, :, h % HH, :], val_ps[:, 0:GT].rearrange("f (b i) -> f b i", b=GB),
                      ACT.Copy).then_inc(val_kept, 1)
                if more:
                    if k == 1:
                        keep_sq(g + 1)
                        keep_hc(g + 1)
                    for h in Z_THEN.get(k, ()):
                        keep_z(g + 1, h, 1 - q)
                if k == 3 and more:
                    keep_xnh(g + 1, 1 - q)

            steps_first(act, step)

            first_part_over(act)

            def keep_aTh(c, j):
                m = AC * c + j
                at_least(act, aT_done, m + 1)
                at_least(act, proj_done, m - 1)
                A(aT_h[:, j % 2], turn_ps[j % 2][:], ACT.Copy).then_inc(aTh_kept, 1)

            def keep_sq2(c):
                at_least(act, hc2_done, c + 1)
                at_least(act, var2_done, c)
                A(sqB[:], hc_ps[:], ACT.Square).then_inc(sq2_kept, 1)
                at_least(act, tok_done, c)
                A(hcB[:], hc_ps[:], ACT.Copy).then_inc(hcs2_kept, 1)

            def keep_trow(c, q):
                at_least(act, trow1_kept, c + 1)
                A(trow[:, q, 1, :, 0:D], trow[:, q, 0, :, 0:D], ACT.Copy).then_inc(trow2_kept, 1)

            def keep_res(c):
                at_least(act, res_done, c + 1)
                dst = h1tok[:, c * RT:(c + 1) * RT] if isinstance(c, int) else h1tok[:, bass.ds(c * RT, RT)]
                A(dst, res_ps[:].rearrange("p (r d) -> p r d", r=RT), ACT.Copy).then_inc(res_kept, 1)

            def keep_gapexp(c):
                at_least(act, gap_kept, c + 1)
                A(top[:, 3], top[:, 2], ACT.Exp).then_inc(gapexp_kept, 1)

            for j in range(AC):
                keep_aTh(0, j)

            def chunk(c, i, q, more):
                for j in range(AC):
                    if more:
                        keep_aTh(c + 1, j)
                    if j == 1:
                        keep_sq2(c)
                    if j == 3:
                        keep_res(c)
                    if j == 6:
                        keep_gapexp(c)
                    if j == 7:
                        keep_trow(c, q)

            steps_second(act, chunk)

            def tile(n, i, q):
                if is_tile(n):
                    at_least(act, xt_done, n + 1)
                    at_least(act, hid_done, n - 1)
                    A(x_h[:, q % 2], xt_ps[:, 0:P], ACT.Copy).then_inc(xh_kept, 1)
                m = n - LAG_R
                if is_tile(m):
                    at_least(act, back_done, m + 1)
                    at_least(act, y_done, m - 1)
                    A(hid_h[:, (q - LAG_R) % 2], back_ps[(q - LAG_R) % 2][:], ACT.Relu).then_inc(hidh_kept, 1)
            tiles(act, tile)

            def send(c, i, q):
                at_least(act, sum2_kept, c + 1)
                sl = slice(c * CT, (c + 1) * CT) if isinstance(c, int) else bass.ds(c * CT, CT)
                act.dma_start(out[sl, :].rearrange("(r p) d -> p r d", p=P), osb[:, q]).then_inc(out_sent[q], 16)

            blocks(act, NCH, FIN, send)
            for q in range(FIN):
                act.wait_ge(out_sent[q], 16 * ((NCH - q + FIN - 1) // FIN))

        @block.vector
        def _(dve):
            V = nc.vector
            dve.wait_ge(cs, 9)
            for j in range(4):
                dve.wait_ge(qkT_done, j + 1)
                V.tensor_copy(raw[0:E, 2048 + 512 * j:2048 + 512 * (j + 1)], bank[j][0:E, :]).then_inc(qkT_kept, 1)
            for j in range(2):
                dve.wait_ge(pair_done, j + 1)
                src = bank[4 + j][:].rearrange("p (h d) -> p h d", h=4)
                V.tensor_copy(pair_h[:, 4 * j:4 * j + 4], src).then_inc(qkT_kept, 1)
                dve.wait_ge(qkT_kept, 5 + j)
                ins = V.tensor_tensor(pair_l[:, 4 * j:4 * j + 4], src, pair_h[:, 4 * j:4 * j + 4].bitcast(F32),
                                      ALU.subtract)
            ins.then_inc(pair_kept, 1)

            def keep_var(g):
                at_least(dve, var_done, g + 1)
                at_least(dve, rstd_kept, g)
                V.tensor_scalar(varA[:], front_ps[0][0:S, 0:GB], EPS, None, ALU.add).then_inc(var_kept, 1)

            def keep_diag(g):
                at_least(dve, rstd_kept, g + 1)
                at_least(dve, spread_done, g)
                V.tensor_tensor(diag[:], ident[0:S, 0:S].unsqueeze(1).to_broadcast([S, GB, S]),
                                rstdA[:].unsqueeze(2).to_broadcast([S, GB, S]), ALU.mult).then_inc(diag_kept, 1)

            def keep_xnT(g, q):
                at_least(dve, spread_done, g + 1)
                at_least(dve, hcs_kept, g + 1)
                at_least(dve, score_done, UN * (g - 1))
                V.tensor_tensor(xnT[:, q], front_ps[0][:, 0:GT], hcA[:], ALU.mult).then_inc(xnT_kept, 1)

            def keep_xtokl(g, q):
                at_least(dve, xtokh_kept, g + 1)
                at_least(dve, mix_done, UN * (g - 1))
                V.tensor_tensor(xtok_l[:, q], front_ps[1][0:S, :].rearrange("t (b d) -> t b d", b=GB),
                                xtok_h[:, q].bitcast(F32), ALU.subtract).then_inc(xtokl_kept, 1)

            keep_var(0)
            keep_diag(0)
            keep_xnT(0, 0)
            keep_xtokl(0, 0)

            dve.wait_ge(ws_small, 4 * 16)
            V.tensor_copy(b2s[0:1, :], b2raw[:]).then_inc(split_b2, 1)
            dve.wait_ge(split_b2, 1)
            V.tensor_tensor(b2_l[:], b2raw[:], b2s[0:1, :].bitcast(F32), ALU.subtract).then_inc(split_b2, 1)
            V.tensor_copy(ones2[:], ones[0:2, :]).then_inc(split_b2, 1)
            V.tensor_copy(ones_r[:], ones[:]).then_inc(split_b2, 1)
            V.tensor_copy(before_r[:], before[:]).then_inc(split_b2, 1)
            dve.wait_ge(ws_lt, 16)
            lt = raw[:, 2 * H * E:2 * H * E + AC * D].rearrange("p (c d) -> p c d", c=AC)
            V.tensor_copy(wlt_h[:], lt).then_inc(split_lt, 1)
            dve.wait_ge(split_lt, 1)
            V.tensor_tensor(wlt_l[:], lt, wlt_h[:].bitcast(F32), ALU.subtract).then_inc(split_lt, 1)
            dve.wait_ge(ws_v, 16)
            V.tensor_copy(wv_h[:], wv_raw).then_inc(split_lt, 1)
            dve.wait_ge(split_lt, 3)
            V.tensor_tensor(wv_l[:], wv_raw, wv_h[:].bitcast(F32), ALU.subtract).then_inc(split_lt, 1)

            def step(g, k, i, q):
                gs, ks = back(g, k, LAG_S)
                if exists(gs):
                    n = UN * gs + ks
                    at_least(dve, exp_kept, n + 1)
                    V.tensor_reduce(total[:, ks % 2], expo[:, ks % 2], AX_X, ALU.add).then_inc(total_kept, 1)
                sc = score_ps[k % 2][0:S, 0:GT].rearrange("i (h j) -> i h j", h=HH)
                if exists(g):
                    n = UN * g + k
                    at_least(dve, score_done, n + 1)
                    V.tensor_reduce(peak[:, k % 2], sc, AX_X, ALU.max).then_inc(peak_kept, 1)
                if exists(gs):
                    n = UN * gs + ks
                    at_least(dve, total_kept, n + 1)
                    at_least(dve, prob_kept, n - 1)
                    V.reciprocal(inv[:, ks % 2], total[:, ks % 2]).then_inc(inv_kept, 1)
                if exists(g):
                    n = UN * g + k
                    at_least(dve, peak_kept, n + 1)
                    at_least(dve, exp_kept, n - 1)
                    V.tensor_tensor(cent[:, k % 2], sc, peak[:, k % 2].unsqueeze(2).to_broadcast([S, HH, S]),
                                    ALU.subtract).then_inc(cent_kept, 1)
                if k == 2 and exists(g + 1):
                    keep_var(g + 1)
                gt, kt = back(g, k, LAG_TK)
                if exists(gt):
                    n = UN * gt + kt
                    at_least(dve, probTh_kept, n + 1)
                    V.tensor_tensor(probT_l[:, kt % 2], probT_ps[kt % 2][0:S, 0:GT].rearrange("j (h i) -> j h i", h=HH),
                                    probT_h[:, kt % 2].bitcast(F32), ALU.subtract).then_inc(probTl_kept, 1)
                if k == 3 and exists(g + 1):
                    keep_xnT(g + 1, 1 - q)
                gm, km = back(g, k, LAG_M)
                if exists(gm):
                    n = UN * gm + km
                    half, b = km // GB, km % GB
                    at_least(dve, mixh_kept, n + 1)
                    V.tensor_tensor(mix_l[:, half * HH:(half + 1) * HH, b, :],
                                    mix_ps[:, 0:GT].rearrange("d (h i) -> d h i", h=HH),
                                    mix_h[:, half * HH:(half + 1) * HH, b, :].bitcast(F32),
                                    ALU.subtract).then_inc(mixl_kept, 1)
                if exists(g + 1):
                    if k == 2:
                        keep_diag(g + 1)
                    if k == 4:
                        keep_xtokl(g + 1, 1 - q)

            steps_first(dve, step)

            first_part_over(dve)

            def keep_aTl(c, j):
                at_least(dve, aTh_kept, AC * c + j + 1)
                at_least(dve, proj_done, AC * c + j - 1)
                V.tensor_tensor(aT_l[:, j % 2], turn_ps[j % 2][:], aT_h[:, j % 2].bitcast(F32),
                                ALU.subtract).then_inc(aTl_kept, 1)

            def keep_h1(c, i, q):
                at_least(dve, proj_done, AC * (c + 1))
                if isinstance(c, int):
                    dve.wait_ge(a_in[q], 32 * (c // 2 + 1))
                else:
                    dve.wait_ge(a_in[q], 16 * (c - q + 2))
                at_least(dve, res_done, c - 1)
                V.tensor_tensor(h1[:, q], proj_ps[:], hch[q][:], ALU.add).then_inc(h1_kept, 1)

            def keep_var2(c):
                at_least(dve, var2_done, c + 1)
                at_least(dve, rstd2_kept, c)
                V.tensor_scalar(varB[:], var_ps[:, 0:RT], EPS, None, ALU.add).then_inc(var2_kept, 1)

            def keep_trow(c, q):
                at_least(dve, tok_done, c + 1)
                at_least(dve, rstd2_kept, c + 1)
                at_least(dve, scattered[q], 16 * 2 * RT * (c // 2) if isinstance(c, int) else 8 * 2 * RT * (c - q))
                dve.wait_ge(goal_kept, SETUP)
                V.tensor_tensor(trow[:, q, 0, :, 0:D], tok_ps[:].rearrange("p (r d) -> p r d", r=RT),
                                rstdB[:, q].unsqueeze(2).to_broadcast([P, RT, D]), ALU.mult).then_inc(trow1_kept, 1)

            NR = 23
            step_no = [0]
            wide = lambda a: a.unsqueeze(2).to_broadcast([P, RT, NE])

            def link(c, ins):
                step_no[0] += 1
                ins.then_inc(route, 1)
                dve.wait_ge(route, NR * c + step_no[0])

            def take_logits(c, q):
                step_no[0] = 0
                at_least(dve, lg_done, c + 1)
                at_least(dve, rstd2_kept, c + 1)
                link(c, V.tensor_tensor(lg[:], count_ps[:, 0:RT * NE].rearrange("p (r e) -> p r e", r=RT),
                                        wide(rstdB[:, q]), ALU.mult))
                link(c, V.tensor_tensor(lg[:], lg[:], brs[:].unsqueeze(1).to_broadcast([P, RT, NE]), ALU.add))

            def largest(c, which, one):
                m, kk = top[:, which], top[:, 4 + which]
                link(c, V.tensor_reduce(m, lg[:], AX_X, ALU.max))
                link(c, V.tensor_tensor(eq[:], lg[:], wide(m), ALU.is_equal))
                link(c, V.tensor_tensor(key[:], eq[:], rank[:], ALU.mult))
                link(c, V.tensor_reduce(kk, key[:], AX_X, ALU.max))
                link(c, V.tensor_tensor(one[:], rank[:], wide(kk), ALU.is_equal))

            def second_largest(c):
                link(c, V.scalar_tensor_tensor(lg[:], one1[:], -3.0e38, lg[:], ALU.mult, ALU.add))
                largest(c, 1, one2)
                at_least(dve, count_done, c)
                V.tensor_tensor(mask[:], one1[:], one2[:], ALU.add).then_inc(mask_kept, 1)
                V.tensor_tensor(top[:, 2], top[:, 1], top[:, 0], ALU.subtract).then_inc(gap_kept, 1)

            def weigh(c):
                at_least(dve, gapexp_kept, c + 1)
                link(c, V.tensor_scalar(top[:, 6], top[:, 3], 1.0, None, ALU.add))
                link(c, V.reciprocal(top[:, 7], top[:, 6]))
                link(c, V.tensor_tensor(top[:, 6], top[:, 7], top[:, 3], ALU.mult))
                dst = wtab[:, :, c * RT:(c + 1) * RT] if isinstance(c, int) else wtab[:, :, bass.ds(c * RT, RT)]
                link(c, V.tensor_copy(dst, top[:, 6:8]))

            def rows_of(c, q):
                at_least(dve, count_done, c + 1)
                dve.wait_ge(goal_kept, SETUP)
                link(c, V.tensor_tensor(place[:], count_ps[:, 64:64 + RT * NE].rearrange("p (r e) -> p r e", r=RT),
                                        base[:].unsqueeze(1).to_broadcast([P, RT, NE]), ALU.add))
                link(c, V.tensor_tensor(base[:], count_ps[:, 128:128 + NE], base[:], ALU.add))
                link(c, V.tensor_tensor(one2[:], one2[:], place[:], ALU.mult))
                link(c, V.tensor_reduce(posf[:, 0], one2[:], AX_X, ALU.add))
                link(c, V.tensor_tensor(one1[:], one1[:], place[:], ALU.mult))
                V.tensor_reduce(posf[:, 1], one1[:], AX_X, ALU.add).then_inc(route, 1)
                assert step_no[0] + 1 == NR, step_no
                at_least(dve, scattered[q], 16 * 2 * RT * (c // 2) if isinstance(c, int) else 8 * 2 * RT * (c - q))
                at_least(dve, route, NR * c + NR)
                V.tensor_copy(posi[:, q], posf[:]).then_inc(posi_kept, 1)

            for j in range(AC):
                keep_aTl(0, j)

            WEIGHED = 17

            def chunk(c, i, q, more):
                keep_h1(c, i, q)
                for j in range(AC):
                    if more:
                        keep_aTl(c + 1, j)
                    if j == 1 and (not isinstance(c, int) or c > 0):
                        step_no[0] = WEIGHED
                        rows_of(c - 1, 1 - q)
                    if j == 3:
                        keep_var2(c)
                    if j == 4:
                        take_logits(c, q)
                        largest(c, 0, one1)
                    if j == 5:
                        second_largest(c)
                        keep_trow(c, q)
                    if j == 7:
                        weigh(c)
                        assert step_no[0] == WEIGHED, step_no

            steps_second(dve, chunk)
            step_no[0] = WEIGHED
            rows_of(NCH - 1, (NCH - 1) % 2)

            done = [0]

            def then(ins):
                done[0] += 1
                ins.then_inc(route, 1)
                dve.wait_ge(route, NR * NCH + done[0])

            then(V.tensor_copy(padi[:], base[0:1, :]))
            then(V.tensor_tensor(held[:], base[0:1, :], ebase[0:1, :], ALU.subtract))
            then(V.tensor_tensor(bound[:], held[:].unsqueeze(2).to_broadcast([1, NE, NT]), bound[:], ALU.is_gt))
            then(V.tensor_reduce(ntile[:], bound[:], AX_X, ALU.add))
            then(V.tensor_scalar(jump[:], ntile[:], -float(P), float(ROOM), ALU.mult, ALU.add))
            then(V.memset(cum[:], 0.0))
            for e in range(NE):
                then(V.tensor_tensor(cum[:, e + 1:e + 2], cum[:, e:e + 1], ntile[:, e:e + 1], ALU.add))
            then(V.memset(whose[:], 0.0))
            then(V.tensor_scalar(where[:], tile_no[:], float(P), None, ALU.mult))
            for e in range(NE):
                then(V.tensor_scalar(past[:], tile_no[:], cum[:, e + 1:e + 2], None, ALU.is_ge))
                then(V.scalar_tensor_tensor(where[:], past[:], jump[:, e:e + 1], where[:], ALU.mult, ALU.add))
                then(V.tensor_tensor(whose[:], whose[:], past[:], ALU.add))
            then(V.tensor_scalar(whose[:], whose[:], float(NE - 1), None, ALU.min))
            then(V.memset(whosei[:], 0))
            then(V.tensor_copy(whosei[:, 4:4 + TILES], whose[:]))
            V.tensor_copy(wherei[:], where[:]).then_inc(table, 1)

            dve.wait_ge(table, 1)
            dve.wait_ge(b1_in, 16)

            experts = {}

            def tile(n, i, q):
                if q == 0:
                    experts["now"] = tile_experts(dve, i)
                if is_tile(n):
                    at_least(dve, xh_kept, n + 1)
                    at_least(dve, hid_done, n - 1)
                    V.tensor_tensor(x_l[:, q % 2], xt_ps[:, 0:P], x_h[:, q % 2].bitcast(F32), ALU.subtract).then_inc(xl_kept, 1)
                m = n - LAG_H
                if is_tile(m):
                    qm = (q - LAG_H) % RING
                    at_least(dve, hid_done, m + 1)
                    at_least(dve, back_done, m - 1)
                    e = experts["now"][4 + q - LAG_H]
                    V.tensor_tensor(pre[:, qm % 2], hid_ps[qm % 2][:], b1b[:, bass.ds(e * FF, FF)], ALU.add).then_inc(pre_kept, 1)
                m = n - LAG_R
                if is_tile(m):
                    qm = (q - LAG_R) % RING
                    at_least(dve, hidh_kept, m + 1)
                    at_least(dve, y_done, m - 1)
                    V.scalar_tensor_tensor(hid_l[:, qm % 2], back_ps[qm % 2][:], 0.0, hid_h[:, qm % 2].bitcast(F32),
                                           ALU.max, ALU.subtract).then_inc(hidl_kept, 1)
                m = n - LAG_Y
                if is_tile(m):
                    qm = (q - LAG_Y) % RING
                    at_least(dve, y_done, m + 1)
                    if isinstance(m, int):
                        at_least(dve, y_out[qm % 4], 16 * (m // 4))
                    else:
                        dve.wait_ge(y_out[qm % 4], 4 * (m - qm % 4))
                    V.tensor_reduce(ytok[:, qm % 4], y_ps[qm % 2][:, 0:2 * D].rearrange("p (h d) -> p d h", h=2),
                                    AX_X, ALU.add).then_inc(y_kept, 1)

            tiles(dve, tile)

            def total_of(c, i, q):
                at_least(dve, y_in[q], 32 * (i + 1))
                at_least(dve, out_sent[q], 16 * i)
                for choice, kept in ((0, sum1_kept), (1, sum2_kept)):
                    if choice == 1:
                        at_least(dve, sum1_kept, c + 1)
                    for r in range(RT):
                        if isinstance(c, int):
                            w, res = wtab[:, choice, c * RT + r:c * RT + r + 1], h1tok[:, c * RT + r]
                        else:
                            w = wtab[:, choice, bass.ds(c * RT + r, 1)]
                            res = h1tok[:, bass.ds(c * RT + r, 1)].rearrange("p o d -> p (o d)")
                        ins = V.scalar_tensor_tensor(osb[:, q, r], yin[:, q, choice, r], w, res if choice == 0 else osb[:, q, r],
                                                     ALU.mult, ALU.add)
                    ins.then_inc(kept, 1)

            dve.wait_ge(res_kept, NCH)
            blocks(dve, NCH, FIN, total_of)

        @block.tensor
        def _(pe):
            pe.wait_ge(cs, 9)
            pe.wait_ge(ws_qk, 32)
            for j in range(4):
                for m in range(4):
                    o = (4 * j + m) * E
                    ins = nc.tensor.transpose(bank[j][0:E, m * D:(m + 1) * D], raw[:, o:o + E], ident[:])
                ins.then_inc(qkT_done, 1)
            pe.wait_ge(qkT_kept, 4)
            for j in range(2):
                for m in range(4):
                    h = 4 * j + m
                    qT = raw[0:E, 2048 + h * D:2048 + (h + 1) * D]
                    kT = raw[0:E, 2048 + (H + h) * D:2048 + (H + h + 1) * D]
                    ins = mm(bank[4 + j][:, m * D:(m + 1) * D], qT, kT, start=True, stop=True)
                ins.then_inc(pair_done, 1)
            pe.wait_ge(pair_kept, 1)
            pe.wait_ge(ws_tok, 16)

            def turn_x(g, c, i, q):
                at_least(pe, z_kept, H * g - 1 + c)
                if c == 0:
                    at_least(pe, x_in[q], 16 * (i + 1))
                for b in range(GB):
                    ins = nc.tensor.transpose(front_ps[c][:, b * NROW:(b + 1) * NROW],
                                              xin[:, q, b, c * P:(c + 1) * P], ident[0:NROW, 0:NROW])
                ins.then_inc(xT_done, 1)

            def embed(g):
                at_least(pe, xT_kept, KC * (g + 1))
                n = 0
                for late in (0, 1):
                    for c in range(KC):
                        ins = mm(front_ps[0][:, 0:GT], tokw[:, late * KC + c], xT[:, c, :, late:late + S],
                                 start=(n == 0), stop=(n == 2 * KC - 1))
                        n += 1
                ins.then_inc(h_done, 1)

            def centre(g):
                at_least(pe, h_kept, g + 1)
                mm(front_ps[1][:, 0:GT], center[:], hT[:], start=True, stop=True).then_inc(hc_done, 1)

            def variance(g):
                at_least(pe, sq_kept, g + 1)
                for b in range(GB):
                    ins = mm(front_ps[0][0:S, b:b + 1], sqA[:, b * S:(b + 1) * S], average[:, 0:1], start=True, stop=True)
                ins.then_inc(var_done, 1)

            def spread(g):
                at_least(pe, diag_kept, g + 1)
                mm(front_ps[0][:, 0:GT], ones[0:S, :], diag[:], start=True, stop=True).then_inc(spread_done, 1)

            def turn_xn(g, q):
                at_least(pe, xnT_kept, g + 1)
                for b in range(GB):
                    ins = nc.tensor.transpose(front_ps[1][0:S, b * D:(b + 1) * D], xnT[:, q, b * S:(b + 1) * S], ident[:])
                ins.then_inc(xn_done, 1)

            def make_z(g, h):
                if h == 0:
                    at_least(pe, xnh_kept, g + 1)
                    at_least(pe, xnl_kept, g + 1)
                if h == 1:
                    at_least(pe, xtokl_kept, g + 1)
                if h >= 2:
                    at_least(pe, z_kept, H * g + h - 1)
                three(front_ps[h % 2][:, 0:GT], pair_h[:, h], pair_l[:, h], xn_h[:], xn_l[:],
                      True, True).then_inc(z_done, 1)

            for c in range(KC):
                turn_x(0, c, 0, 0)
            embed(0)
            centre(0)
            variance(0)
            spread(0)
            turn_xn(0, 0)
            for h in range(H):
                make_z(0, h)

            def step(g, k, i, q):
                more = exists(g + 1)
                if exists(g):
                    n = UN * g + k
                    half, b = k // GB, k % GB
                    at_least(pe, z_kept, H * g + (half + 1) * HH)
                    at_least(pe, cent_kept, n - 1)
                    mm(score_ps[k % 2][0:S, 0:GT], xnT[:, q, b * S:(b + 1) * S], z[:, q, b, half * HH:(half + 1) * HH, :],
                       start=True, stop=True).then_inc(score_done, 1)
                if more:
                    if k == 0:
                        turn_x(g + 1, 0, i + q, 1 - q)
                    if k == 1:
                        embed(g + 1)
                    if k == 2:
                        variance(g + 1)
                    if k == 4:
                        turn_xn(g + 1, 1 - q)
                    for h in Z_FIRST.get(k, ()):
                        make_z(g + 1, h)
                gm, km = back(g, k, LAG_M)
                if exists(gm):
                    n = UN * gm + km
                    qm = q if k >= LAG_M else 1 - q
                    at_least(pe, probTl_kept, n + 1)
                    at_least(pe, xtokl_kept, gm + 1)
                    at_least(pe, mixl_kept, n)
                    three(mix_ps[:, 0:GT], xtok_h[:, qm, km % GB], xtok_l[:, qm, km % GB],
                          probT_h[:, km % 2], probT_l[:, km % 2], True, True).then_inc(mix_done, 1)
                gt, kt = back(g, k, LAG_T)
                if exists(gt):
                    n = UN * gt + kt
                    at_least(pe, prob_kept, n + 1)
                    at_least(pe, probTl_kept, n - 1)
                    for m in range(HH):
                        ins = nc.tensor.transpose(probT_ps[kt % 2][0:S, m * S:(m + 1) * S], prob[:, kt % 2, m], ident[0:S, 0:S])
                    ins.then_inc(probT_done, 1)
                gv, h = back(g, k, LAG_V)
                if exists(gv):
                    at_least(pe, mixl_kept, UN * gv + (h // HH + 1) * GB)
                    at_least(pe, val_kept, H * gv + h)
                    three(val_ps[:, 0:GT], wv_h[:, h], wv_l[:, h], mix_h[:, h], mix_l[:, h], True, True).then_inc(val_done, 1)
                if more:
                    if k == 0:
                        turn_x(g + 1, 1, i + q, 1 - q)
                    if k == 1:
                        centre(g + 1)
                    if k == 3:
                        spread(g + 1)
                    for h in Z_THEN.get(k, ()):
                        make_z(g + 1, h)

            pe.wait_ge(split_lt, 4)
            steps_first(pe, step)

            first_part_over(pe)
            pe.wait_ge(split_lt, 2)
            pe.wait_ge(split_b2, 5)
            pe.wait_ge(b2_moved, 16)

            def turn_a(c, j, q):
                m = AC * c + j
                if j == 0:
                    if isinstance(c, int):
                        pe.wait_ge(a_in[q], 32 * (c // 2 + 1))
                    else:
                        pe.wait_ge(a_in[q], 16 * (c - q + 2))
                at_least(pe, aTl_kept, m - 1)
                for r in range(RT):
                    ins = nc.tensor.transpose(turn_ps[j % 2][:, r * P:(r + 1) * P], arow[q][:, r, j * P:(j + 1) * P], ident[:])
                ins.then_inc(aT_done, 1)

            def project(c, j):
                m = AC * c + j
                if j == 0:
                    at_least(pe, h1_kept, c)
                at_least(pe, aTh_kept, m + 1)
                at_least(pe, aTl_kept, m + 1)
                three(proj_ps[:], wlt_h[:, j], wlt_l[:, j], aT_h[:, j % 2], aT_l[:, j % 2],
                      j == 0, j == AC - 1).then_inc(proj_done, 1)

            def centre2(c, q):
                at_least(pe, h1_kept, c + 1)
                at_least(pe, hcs2_kept, c)
                mm(hc_ps[:], center[:], h1[:, q], start=True, stop=True).then_inc(hc2_done, 1)

            def variance2(c):
                at_least(pe, sq2_kept, c + 1)
                at_least(pe, var2_kept, c)
                for r in range(RT):
                    ins = mm(var_ps[:, r:r + 1], sqB[:, r * P:(r + 1) * P], average[:, 0:1], start=True, stop=True)
                ins.then_inc(var2_done, 1)

            def logits(c):
                at_least(pe, hcs2_kept, c + 1)
                at_least(pe, posi_kept, c)
                for r in range(RT):
                    ins = mm(count_ps[:, r * NE:(r + 1) * NE], hcB[:, r * P:(r + 1) * P], wrs[:], start=True, stop=True)
                ins.then_inc(lg_done, 1)

            def turn_tok(c):
                at_least(pe, trow1_kept, c)
                for r in range(RT):
                    ins = nc.tensor.transpose(tok_ps[:, r * D:(r + 1) * D], hcB[:, r * P:(r + 1) * P], ident[:])
                ins.then_inc(tok_done, 1)

            def turn_res(c, q):
                at_least(pe, res_kept, c)
                for r in range(RT):
                    ins = nc.tensor.transpose(res_ps[:, r * D:(r + 1) * D], h1[:, q, r * P:(r + 1) * P], ident[:])
                ins.then_inc(res_done, 1)

            def count(c):
                at_least(pe, mask_kept, c + 1)
                m2 = mask[:].rearrange("p r e -> p (r e)")
                for back_by in range(RT):
                    n = (RT - back_by) * NE
                    mm(count_ps[:, 64 + back_by * NE:64 + RT * NE], before_r[:] if back_by == 0 else ones_r[:], m2[:, 0:n],
                       start=back_by == 0, stop=back_by == RT - 1)
                for r in range(RT):
                    ins = mm(count_ps[:, 128:128 + NE], ones_r[:], mask[:, r], start=r == 0, stop=r == RT - 1)
                ins.then_inc(count_done, 1)

            for j in range(AC):
                turn_a(0, j, 0)
                if j:
                    project(0, j - 1)
            project(0, AC - 1)

            def chunk(c, i, q, more):
                for j in range(AC + 1):
                    if j == 3:
                        variance2(c)
                    if more and j < AC:
                        turn_a(c + 1, j, 1 - q)
                    if j == 1:
                        centre2(c, q)
                    if j == 4:
                        logits(c)
                    if j == AC:
                        count(c)
                    if more and j:
                        project(c + 1, j - 1)
                    if j == 2:
                        turn_res(c, q)
                    if j == 4:
                        turn_tok(c)

            steps_second(pe, chunk)

            pe.wait_ge(table, 1)
            pe.wait_ge(split_12, 16)
            pe.wait_ge(posi_kept, NCH)
            pe.wait_ge(trow1_kept, NCH)
            pe.wait_ge(res_kept, NCH)

            experts = {}

            def tile(n, i, q):
                if q == 0:
                    experts["now"] = tile_experts(pe, i)
                if is_tile(n):
                    at_least(pe, tile_in[q], 16 * (i + 1))
                    at_least(pe, xl_kept, n)
                    nc.tensor.transpose(xt_ps[:, 0:P], tin[:, q, 0:D], ident[:]).then_inc(xt_done, 1)
                m = n - LAG_H
                if is_tile(m):
                    b = (q - LAG_H) % 2
                    e = experts["now"][4 + q - LAG_H]
                    at_least(pe, xl_kept, m + 1)
                    at_least(pe, pre_kept, m - 1)
                    high, low = w1_h[:, bass.ds(e * FF, FF)], w1_l[:, bass.ds(e * FF, FF)]
                    mm(hid_ps[b][:], x_h[:, b], high, start=True, stop=False)
                    mm(hid_ps[b][:], x_l[:, b], high, start=False, stop=False)
                    mm(hid_ps[b][:], x_h[:, b], low, start=False, stop=True).then_inc(hid_done, 1)
                m = n - LAG_R
                if is_tile(m):
                    b = (q - LAG_R) % 2
                    at_least(pe, pre_kept, m + 1)
                    at_least(pe, hidl_kept, m - 1)
                    for f in range(FC):
                        ins = nc.tensor.transpose(back_ps[b][:, f * P:(f + 1) * P], pre[:, b, f * P:(f + 1) * P], ident[:])
                    ins.then_inc(back_done, 1)
                m = n - LAG_Y
                if is_tile(m):
                    b = (q - LAG_Y) % 2
                    e = experts["now"][4 + q - LAG_Y]
                    at_least(pe, hidl_kept, m + 1)
                    at_least(pe, y_kept, m - 1)
                    weights = w2s[:].rearrange("p a h d -> p (a h d)")
                    for f in range(FC):
                        at = e * (FC * 2 * D) + f * 2 * D
                        hh, hl = hid_h[:, b, f * P:(f + 1) * P], hid_l[:, b, f * P:(f + 1) * P]
                        mm(y_ps[b][:, 0:2 * D], hh, weights[:, bass.ds(at, 2 * D)], start=f == 0, stop=False,
                           skip_group_check=True)
                        mm(y_ps[b][:, 0:D], hl, weights[:, bass.ds(at, D)], start=False, stop=False, skip_group_check=True)
                    mm(y_ps[b][:, 0:D], ones2[:], b2s[:, bass.ds(e * D, D)], start=False, stop=True,
                       skip_group_check=True).then_inc(y_done, 1)

            tiles(pe, tile)


_INS = ['x', 'L0_tok_W', 'L0_tok_b', 'L0_attn_Wq', 'L0_attn_Wk', 'L0_attn_Wv', 'L0_attn_Wlt', 'L0_ffn_Wr',
        'L0_ffn_br', 'L0_ffn_W1', 'L0_ffn_b1', 'L0_ffn_W2', 'L0_ffn_b2']


def kernel(**inputs):
    import numpy as _np
    import concourse.bacc as _bacc
    from concourse import mybir as _mybir
    from concourse.bass_utils import run_bass_kernel_spmd as _run

    nc = _bacc.Bacc("TRN2", target_bir_lowering=False, num_devices=1)
    arrays, args = {}, []
    for name in _INS:
        a = _np.ascontiguousarray(inputs[name])
        arrays[f"in_{name}_dram"] = a
        args.append(nc.dram_tensor(f"in_{name}_dram", a.shape, _mybir.dt.from_np(a.dtype), kind="ExternalInput").ap())
    args.append(nc.dram_tensor("out_0_dram", (T, D), F32, kind="ExternalOutput").ap())
    build(nc, *args)
    r = _run(nc, [arrays], core_ids=[0])
    return r.results[0]["out_0_dram"].reshape(B, S, D)
```

```python
from contextlib import ExitStack

import concourse.bass as bass
from concourse import mybir

ALU = mybir.AluOpType
ACT = mybir.ActivationFunctionType
F32 = mybir.dt.float32
F32R = mybir.dt.float32r
I32 = mybir.dt.int32
AX_X = mybir.AxisListType.X

P = 128
B, L, FEAT = 128, 750, 32
PATCH, STRIDE = 16, 8
S = (L - PATCH) // STRIDE + 1
D = 128
H, E = 8, 64
NE, FF = 8, 512
FC = FF // P
EPS = 1e-5
T = B * S
ROW = STRIDE * FEAT
NROW = S + 1
KC = ROW // P

GB = 4
NG = B // GB
GT = GB * S
HH = H // 2
UN = 2 * GB
LAG_S, LAG_T, LAG_TK, LAG_M, LAG_V = 1, 2, 3, 4, 8

CT = 512
NCH = T // CT
RT = CT // P
NT = T // P
TURNS = 4
LAG_P = 2
AC = H * D // P

ROWW = D + 4
ROOM = T + P
TILES = 2 * NT + NE
SPARE = TILES - 2 * NT
SORTED_ROWS = NE * ROOM + SPARE * P
HT = TILES // 2
CEIL = -(-SPARE * ROWW // D)
Y_ROWS = 2 * T + (NE + SPARE) * P
RING = 8
LAG_H, LAG_R, LAG_Y = 1, 2, 3
SETUP = 10
FIN = 4
assert TILES % RING == 0 and T % CT == 0 and GT <= 512 and HH * S == GT and H * S * D == S * H * D


def at_least(eng, sem, value):
    if isinstance(value, int) and value <= 0:
        return
    eng.wait_ge(sem, value)


def back(g, k, lag):
    k -= lag
    while k < 0:
        g, k = g - 1, k + UN
    return g, k


def exists(g):
    return not isinstance(g, int) or 0 <= g < NG


def build(nc, x, tok_w, tok_b, wq, wk, wv, wlt, wr, br, w1, b1, w2, b2, out):
    ax_dram = nc.dram_tensor("ax_scratch", (T * H * D,), F32, kind="Internal").ap()
    h_dram = nc.dram_tensor("h_scratch", (D, T), F32, kind="Internal").ap()
    sorted_dram = nc.dram_tensor("sorted_scratch", (SORTED_ROWS, ROWW), F32, kind="Internal").ap()
    y_dram = nc.dram_tensor("y_scratch", (Y_ROWS, D), F32, kind="Internal").ap()
    ax_in = ax_dram.rearrange("(b f h i) -> b f h i", f=D, h=H, i=S)
    ax_rows = ax_dram.rearrange("(t c) -> t c", c=H * D)
    x_rows = x.rearrange("b l f -> b (l f)")

    with ExitStack() as ctx, nc.allow_non_contiguous_dma("biases once"):
        def sb(name, shape, dt=F32, stack=ctx):
            return stack.enter_context(nc.sbuf_tensor(name, shape, dt))

        def sem(name):
            return ctx.enter_context(nc.semaphore(name))

        ident = sb("ident", [P, P])
        center = sb("center", [P, P])
        average = sb("average", [P, P])
        ones = sb("ones", [P, P])
        before = sb("before", [P, P])
        wlt_h = sb("wlt_h", [P, AC, D], F32R)
        wlt_l = sb("wlt_l", [P, AC, D], F32R)
        w1_h = sb("w1_h", [D, NE * FF], F32R)
        w1_l = sb("w1_l", [D, NE * FF], F32R)
        loading = ExitStack()
        w2raw = sb("w2raw", [P, NE * FC, 2, D], stack=loading)
        loading.close()
        w2s = sb("w2s", [P, NE * FC, 2, D], F32R)
        wrs = sb("wrs", [D, NE])
        brs = sb("brs", [P, NE])
        before_r = sb("before_r", [P, P], F32R)
        ones_r = sb("ones_r", [P, P], F32R)
        power = sb("power", [P, GB])
        ones2 = sb("ones2", [2, P], F32R)
        b2s = sb("b2s", [2, NE * D], F32R)
        rank = sb("rank", [P, RT, NE])

        arow0 = sb("arow0", [P, RT, H * D])
        raw = arow0[:].rearrange("p r n -> p (r n)")
        hch0 = sb("hch0", [D, CT])

        first = ExitStack()
        tokw = sb("tokw", [P, 2 * KC, D], stack=first)
        tokb = sb("tokb", [D, 1], stack=first)
        pair_h = sb("pair_h", [D, H, D], F32R, stack=first)
        pair_l = sb("pair_l", [D, H, D], F32R, stack=first)
        wv_h = sb("wv_h", [D, H, D], F32R, stack=first)
        wv_l = sb("wv_l", [D, H, D], F32R, stack=first)
        b2raw = sb("b2raw", [1, NE * D], stack=first)
        b2_l = sb("b2_l", [1, NE * D], F32R, stack=first)
        xin = sb("xin", [NROW, 2, GB, ROW], stack=first)
        xT = sb("xT", [P, KC, GB, NROW], stack=first)
        hT = sb("hT", [D, GT], stack=first)
        sqA = sb("sqA", [D, GT], stack=first)
        hcA = sb("hcA", [D, GT], stack=first)
        varA = sb("varA", [S, GB], stack=first)
        rstdA = sb("rstdA", [S, GB], stack=first)
        diag = sb("diag", [S, GB, S], stack=first)
        xnT = sb("xnT", [D, 2, GT], stack=first)
        xn_h = sb("xn_h", [D, GT], F32R, stack=first)
        xn_l = sb("xn_l", [D, GT], F32R, stack=first)
        xtok_h = sb("xtok_h", [S, 2, GB, D], F32R, stack=first)
        xtok_l = sb("xtok_l", [S, 2, GB, D], F32R, stack=first)
        z = sb("z", [D, 2, GB, H, S], stack=first)
        peak = sb("peak", [S, 2, HH], stack=first)
        cent = sb("cent", [S, 2, HH, S], stack=first)
        expo = sb("expo", [S, 2, HH, S], stack=first)
        total = sb("total", [S, 2, HH], stack=first)
        inv = sb("inv", [S, 2, HH], stack=first)
        prob = sb("prob", [S, 2, HH, S], stack=first)
        probT_h = sb("probT_h", [S, 2, HH, S], F32R, stack=first)
        probT_l = sb("probT_l", [S, 2, HH, S], F32R, stack=first)
        mix_room = w2s[:].rearrange("p a h d -> p (a h d)")
        mix_h, mix_l = (mix_room[:, j * H * GT:(j + 1) * H * GT].rearrange("d (h b i) -> d h b i", h=H, b=GB)
                        for j in (0, 1))
        val = sb("val", [D, 2, GB, HH, S], stack=first)
        wv_raw = val[:].rearrange("d a b h i -> d (a b h i)")[:, 0:H * D].rearrange("d (h f) -> d h f", h=H)
        first.close()

        h1tok = sb("h1tok", [P, NT, D])
        wtab = sb("wtab", [P, 2, NT])

        padi = sb("padi", [1, NE], I32)
        whosei = sb("whosei", [1, TILES + 12], I32)
        wherei = sb("wherei", [1, TILES], I32)
        goals = sb("goals", [P, RING], I32)

        second = ExitStack()
        arow = [arow0, sb("arow1", [P, RT, H * D], stack=second)]
        hch = [hch0, sb("hch1", [D, CT], stack=second)]
        aT_h = sb("aT_h", [P, TURNS, CT], F32R, stack=second)
        aT_l = sb("aT_l", [P, TURNS, CT], F32R, stack=second)
        h1 = sb("h1", [D, 2, CT], stack=second)
        sqB = sb("sqB", [D, CT], stack=second)
        hcB = sb("hcB", [D, CT], stack=second)
        varB = sb("varB", [P, RT], stack=second)
        rstdB = sb("rstdB", [P, 2, RT], stack=second)
        lg = sb("lg", [P, RT, NE], stack=second)
        eq = sb("eq", [P, RT, NE], stack=second)
        key = sb("key", [P, RT, NE], stack=second)
        one1 = sb("one1", [P, RT, NE], stack=second)
        one2 = sb("one2", [P, RT, NE], stack=second)
        mask = sb("mask", [P, RT, NE], F32R, stack=second)
        place = sb("place", [P, RT, NE], stack=second)
        top = sb("top", [P, 8, RT], stack=second)
        base = sb("base", [P, NE], stack=second)
        posf = sb("posf", [P, 2, RT], stack=second)
        posi = sb("posi", [P, 2, 2, RT], I32, stack=second)
        goal = sb("goal", [P, 2, RT], stack=second)
        trow = sb("trow", [P, 2, 2, RT, ROWW], stack=second)
        blank = sb("blank", [P, NE, ROWW], stack=second)
        ebase = sb("ebase", [P, NE], stack=second)
        held = sb("held", [P, NE], stack=second)
        starts = sb("starts", [P, 1], stack=second)
        holds = sb("holds", [P, NE], stack=second)
        jump = sb("jump", [P, NE], stack=second)
        tile_no = sb("tile_no", [HT, 2], stack=second)
        past = sb("past", [HT, 2, NE], stack=second)
        jumps = sb("jumps", [HT, 2, NE], stack=second)
        ahead = sb("ahead", [HT, 2], stack=second)
        entry = sb("entry", [HT, 2, 2], stack=second)
        second.close()
        spare_rows = h1tok[:, NT - CEIL:NT].rearrange("p n d -> p (n d)")[:, 0:SPARE * ROWW].rearrange(
            "p (k w) -> p k w", k=SPARE)

        third = ExitStack()
        b1b = sb("b1b", [P, NE * FF], stack=third)
        tin = sb("tin", [P, RING, ROWW], stack=third)
        x_h = sb("x_h", [D, 2, P], F32R, stack=third)
        x_l = sb("x_l", [D, 2, P], F32R, stack=third)
        pre = sb("pre", [P, 2, FF], stack=third)
        hid_h = sb("hid_h", [P, 2, FF], F32R, stack=third)
        hid_l = sb("hid_l", [P, 2, FF], F32R, stack=third)
        ytok = sb("ytok", [P, 4, D], stack=third)
        yin = sb("yin", [P, FIN, 2, RT, D], stack=third)
        osb = sb("osb", [P, FIN, RT, D], stack=third)
        third.close()

        bank = [ctx.enter_context(nc.psum_tensor(f"bank{i}", [P, 512], F32)) for i in range(8)]
        front_ps, score_ps, probT_ps, mix_ps, val_ps = bank[0:2], bank[2:4], bank[4:6], bank[6], bank[7]
        turn_ps, proj_ps, tok_ps, res_ps = (bank[0], bank[1], bank[4], bank[7]), bank[2], bank[3], bank[3]
        count_ps, hc_ps = bank[5], bank[6]
        var_ps = count_ps[:, 192:192 + RT]
        cum_ps, ntile_ps, row_ps = res_ps[:, 0:NE], res_ps[:, 64:64 + NE], hc_ps[0:1, 0:2 * TILES]
        xt_ps, hid_ps, back_ps, y_ps = bank[0], bank[1:3], bank[3:5], bank[5:7]

        ws_small, ws_tok, ws_qk, ws_v, ws_lt, ws_1, ws_2 = (sem(n) for n in (
            "ws_small", "ws_tok", "ws_qk", "ws_v", "ws_lt", "ws_1", "ws_2"))
        cs = sem("cs")
        qkT_done, qkT_kept, pair_done, pair_kept = (sem(n) for n in ("qkT_done", "qkT_kept", "pair_done", "pair_kept"))
        split_v, split_lt, high_kept, low_kept, split_b2, b2_moved = (sem(n) for n in (
            "split_v", "split_lt", "high_kept", "low_kept", "split_b2", "b2_moved"))
        x_in = [sem("x_in0"), sem("x_in1")]
        xT_done, xT_kept, h_done, h_kept, h_out = (sem(n) for n in ("xT_done", "xT_kept", "h_done", "h_kept", "h_out"))
        hc_done, sq_kept, hcs_kept, var_done, var_kept, rstd_kept, diag_kept, spread_done = (sem(n) for n in (
            "hc_done", "sq_kept", "hcs_kept", "var_done", "var_kept", "rstd_kept", "diag_kept", "spread_done"))
        xnT_kept, xnh_kept, xnl_kept, xn_done, xtokh_kept, xtokl_kept = (sem(n) for n in (
            "xnT_kept", "xnh_kept", "xnl_kept", "xn_done", "xtokh_kept", "xtokl_kept"))
        z_done, z_kept = sem("z_done"), sem("z_kept")
        score_done, peak_kept, cent_kept, exp_kept, total_kept, inv_kept = (sem(n) for n in (
            "score_done", "peak_kept", "cent_kept", "exp_kept", "total_kept", "inv_kept"))
        prob_kept, probT_done, probTh_kept, probTl_kept = (sem(n) for n in (
            "prob_kept", "probT_done", "probTh_kept", "probTl_kept"))
        mix_done, mixh_kept, mixl_kept, val_done, val_kept = (sem(n) for n in (
            "mix_done", "mixh_kept", "mixl_kept", "val_done", "val_kept"))
        val_out = [sem("val_out0"), sem("val_out1")]
        a_in = [sem("a_in0"), sem("a_in1")]
        aT_done, aTh_kept, aTl_kept, proj_done, h1_kept = (sem(n) for n in (
            "aT_done", "aTh_kept", "aTl_kept", "proj_done", "h1_kept"))
        hc2_done, sq2_kept, hcs2_kept, var2_done, var2_kept, rstd2_kept = (sem(n) for n in (
            "hc2_done", "sq2_kept", "hcs2_kept", "var2_done", "var2_kept", "rstd2_kept"))
        lg_done, route, mask_kept, gap_kept, gapexp_kept, count_done, posi_kept = (sem(n) for n in (
            "lg_done", "route", "mask_kept", "gap_kept", "gapexp_kept", "count_done", "posi_kept"))
        tok_done, trow_kept, res_done, res_kept, goal_kept = (sem(n) for n in (
            "tok_done", "trow_kept", "res_done", "res_kept", "goal_kept"))
        scattered = [sem("scattered0"), sem("scattered1")]
        passed, counted, entries_kept, listed = (sem(n) for n in ("passed", "counted", "entries_kept", "listed"))
        padi_kept, holds_kept = sem("padi_kept"), sem("holds_kept")
        table, pads_in, spares_in, b1_in = (sem(n) for n in ("table", "pads_in", "spares_in", "b1_in"))
        tile_in = [sem(f"tile_in{i}") for i in range(RING)]
        xt_done, xh_kept, xl_kept, goal_read = (sem(n) for n in ("xt_done", "xh_kept", "xl_kept", "goal_read"))
        hid_done, pre_kept, back_done, hidh_kept, hidl_kept, y_done, y_kept = (sem(n) for n in (
            "hid_done", "pre_kept", "back_done", "hidh_kept", "hidl_kept", "y_done", "y_kept"))
        y_out = [sem(f"y_out{i}") for i in range(4)]
        y_in = [sem(f"y_in{i}") for i in range(FIN)]
        scaled, sum1_kept, sum2_kept = sem("scaled"), sem("sum1_kept"), sem("sum2_kept")
        out_sent = [sem(f"out_sent{i}") for i in range(FIN)]

        Z_FIRST = {5: (1,), 6: (3,), 7: (6,)}
        Z_THEN = {4: (0,), 5: (2,), 6: (4, 5), 7: (7,)}

        NR = 23

        block = ctx.enter_context(nc.Block())
        mm = nc.tensor.matmul

        def three(dst, wh, wl, vh, vl, start, stop):
            mm(dst, wh, vh, start=start, stop=False)
            mm(dst, wh, vl, start=False, stop=False)
            return mm(dst, wl, vh, start=False, stop=stop)

        def steps_first(eng, step):
            for g in (0, 1):
                for k in range(UN):
                    step(g, k, 0, g)
            with eng.Fori(1, NG // 2 - 1) as i:
                for q in (0, 1):
                    for k in range(UN):
                        step(2 * i + q, k, i, q)
            for g in (NG - 2, NG - 1):
                for k in range(UN):
                    step(g, k, NG // 2 - 1, g % 2)
            for k in range(LAG_V):
                step(NG, k, NG // 2, 0)

        def steps_second(eng, chunk):
            chunk(0, 0, 0, True)
            chunk(1, 0, 1, True)
            chunk(2, 1, 0, True)
            with eng.Fori(1, (NCH - 3) // 2) as i:
                chunk(2 * i + 1, i, 1, True)
                chunk(2 * i + 2, i + 1, 0, True)
            chunk(NCH - 2, (NCH - 3) // 2, 1, True)
            chunk(NCH - 1, (NCH - 1) // 2, 0, False)

        def blocks(eng, total, size, step):
            for n in range(size):
                step(n, 0, n)
            with eng.Fori(1, total // size) as i:
                for q in range(size):
                    step(size * i + q, i, q)
            for n in range(total // size * size, total):
                step(n, n // size, n % size)

        def tiles(eng, step):
            blocks(eng, TILES, RING, step)
            for n in range(TILES, TILES + LAG_Y + 1):
                step(n, n // RING, n % RING)

        def tile_experts(eng, i):
            sl = slice(RING * i, RING * i + 12) if isinstance(i, int) else bass.ds(RING * i, 12)
            regs = expert_regs[eng.engine]
            eng.load(regs, whosei[0:1, sl])
            return [eng.snap(r, min_val=0, max_val=NE - 1) for r in regs]

        expert_regs = {eng.engine: [eng.alloc_register(f"expert{j}") for j in range(12)] for eng in (nc.tensor, nc.vector)}

        def is_tile(n):
            return not isinstance(n, int) or 0 <= n < TILES

        def pool_waits(*waits):
            for sm, v in waits:
                at_least(nc.gpsimd, sm, v)
            nc.gpsimd.sem_inc(passed, 1)

        def weight_of(choice, c, r):
            at = c * RT + r
            return wtab[:, choice, at:at + 1] if isinstance(c, int) else wtab[:, choice, bass.ds(at, 1)]

        def lay_pads(eng, experts):
            eng.wait_ge(padi_kept, 1)
            for e in experts:
                row = eng.value_load(padi[0:1, e:e + 1], min_val=e * ROOM, max_val=e * ROOM + T)
                eng.dma_start(sorted_dram[bass.ds(row, P), :], blank[:, e]).then_inc(pads_in, 16)

        def first_part_computed(eng):
            eng.wait_ge(h_out, 16 * NG)
            eng.wait_ge(val_kept, H * NG)

        def first_part_over(eng):
            eng.wait_ge(h_out, 16 * NG)
            for half in (0, 1):
                eng.wait_ge(val_out[half], 16 * NG)

        @block.sync
        def _(sp):

            def load_x(g, i, q):
                at_least(sp, xT_done, KC * (g - 1))
                if isinstance(g, int):
                    src = x_rows[g * GB:(g + 1) * GB, 0:NROW * ROW]
                else:
                    src = x_rows[bass.ds(g * GB, GB), 0:NROW * ROW]
                sp.dma_start(xin[:, q], src.rearrange("b (r c) -> r b c", c=ROW)).then_inc(x_in[q], 16)

            def store_h(g):
                at_least(sp, h_kept, g + 1)
                dst = h_dram[:, g * GT:(g + 1) * GT] if isinstance(g, int) else h_dram[:, bass.ds(g * GT, GT)]
                sp.dma_start(dst, hT[:]).then_inc(h_out, 16)

            def load_a(c, i, q):
                at_least(sp, aT_done, AC * (c - 1))
                at_least(sp, h1_kept, c - 1)
                if isinstance(c, int):
                    rows, cols = ax_rows[c * CT:(c + 1) * CT, :], h_dram[:, c * CT:(c + 1) * CT]
                else:
                    rows, cols = ax_rows[bass.ds(c * CT, CT), :], h_dram[:, bass.ds(c * CT, CT)]
                sp.dma_start(arow[q][:], rows.rearrange("(r p) n -> p r n", p=P)).then_inc(a_in[q], 16)
                sp.dma_start(hch[q][:], cols).then_inc(a_in[q], 16)

            load_x(0, 0, 0)
            sp.dma_start(tokw[:], tok_w.rearrange("(c p) d -> p c d", p=P)).then_inc(ws_tok, 16)
            sp.dma_start(wv_raw, wv.rearrange("h d f -> d h f")).then_inc(ws_v, 16)
            load_x(1, 0, 1)
            store_h(0)

            def step(g, k, i, q):
                nxt = g + 1
                if k == 2 and exists(g + 2):
                    load_x(g + 2, i + 1, q)
                if k == 3 and exists(nxt):
                    store_h(nxt)
                if isinstance(g, int) and g == NG - 1 and k == 0:
                    sp.wait_ge(low_kept, NE)
                    for half in (0, 1):
                        sp.wait_ge(val_out[half], 16 * (CT // GT + 1))
                    load_a(0, 0, 0)
                gv, h = back(g, k, LAG_V)
                if h % HH == HH - 1 and exists(gv):
                    half = h // HH
                    at_least(sp, val_kept, H * gv + h + 1)
                    dst = ax_in[gv * GB:(gv + 1) * GB] if isinstance(gv, int) else ax_in[bass.ds(gv * GB, GB)]
                    sp.dma_start(dst[:, :, half * HH:(half + 1) * HH, :].rearrange("b f h i -> f b (h i)"),
                                 val[:, half].rearrange("f b h i -> f b (h i)")).then_inc(val_out[half], 16)

            steps_first(sp, step)

            first_part_computed(sp)
            load_a(1, 0, 1)
            first_part_over(sp)

            def chunk(c, i, q, more):
                if not isinstance(c, int) or c + 2 < NCH:
                    load_a(c + 2, i + 1, q)

            steps_second(sp, chunk)

            sp.wait_ge(aT_done, AC * (NCH - 1))
            sp.dma_start(b1b[:], b1.rearrange("e f -> (e f)").partition_broadcast(P)).then_inc(b1_in, 16)
            lay_pads(sp, range(0, NE, 2))
            sp.wait_ge(table, 1)
            sp.wait_ge(pads_in, 16 * NE)
            sp.wait_ge(spares_in, 16 * SPARE)
            for half in (0, 1):
                sp.wait_ge(scattered[half], 16 * 2 * RT * ((NCH + 1 - half) // 2))

            def load_tile(n, i, q):
                at_least(sp, xt_done, n - RING + 1)
                at_least(sp, goal_read, n - RING + 1)
                row = sp.value_load(wherei[0:1, bass.ds(n, 1)], min_val=0, max_val=SORTED_ROWS - P)
                sp.dma_start(tin[:, q], sorted_dram[bass.ds(row, P), :]).then_inc(tile_in[q], 16)

            blocks(sp, TILES, RING, load_tile)

            for j in range(4):
                sp.wait_ge(y_out[j], 16 * (TILES // 4))

            def rows(ap, c, first):
                sl = slice(first + c * CT, first + (c + 1) * CT) if isinstance(c, int) else bass.ds(c * CT + first, CT)
                return ap[sl, :].rearrange("(r p) d -> p r d", p=P)

            def load_y(c, i, q):
                at_least(sp, sum2_kept, c - FIN + 1)
                for choice in (0, 1):
                    sp.dma_start(yin[:, q, choice], rows(y_dram, c, (1 - choice) * T)).then_inc(y_in[q], 16)

            blocks(sp, NCH, FIN, load_y)
            sp.wait_ge(sum2_kept, NCH)

        @block.gpsimd
        def _(pool):
            count = [0]

            def const(ins):
                count[0] += 1
                ins.then_inc(cs, 1)
                return count[0]

            const(pool.memset(ident[:], 0.0))
            const(pool.memset(average[:], 1.0 / D))
            const(pool.memset(center[:], -1.0 / D))
            const(pool.memset(power[:], -0.5))
            const(pool.memset(ones[:], 1.0))
            const(pool.memset(before[:], 1.0))
            pool.wait_ge(cs, count[0])
            const(pool.affine_select(out=ident[:], in_=ident[:], compare_op=ALU.not_equal, fill=1.0, base=0,
                                     pattern=[[-1, P]], channel_multiplier=1))
            const(pool.affine_select(out=center[:], in_=center[:], compare_op=ALU.not_equal, fill=1.0 - 1.0 / D,
                                     base=0, pattern=[[-1, P]], channel_multiplier=1))
            const(pool.affine_select(out=before[:], in_=before[:], compare_op=ALU.is_gt, fill=0.0, base=0,
                                     pattern=[[1, P]], channel_multiplier=-1))
            assert count[0] == 9
            for e in range(NE):
                const(pool.memset(rank[:, :, e:e + 1], float(NE - e)))

            def low_w(src, high, low, n):
                pool.wait_ge(high_kept, n + 1)
                nc.gpsimd.tensor_tensor(low, src, high.bitcast(F32), ALU.subtract).then_inc(low_kept, 1)

            def scale_prob(g, k):
                n = UN * g + k
                at_least(pool, inv_kept, n + 1)
                at_least(pool, exp_kept, n + 1)
                at_least(pool, probT_done, n - 1)
                nc.gpsimd.tensor_tensor(prob[:, k % 2], expo[:, k % 2],
                                        inv[:, k % 2].unsqueeze(2).to_broadcast([S, HH, S]), ALU.mult).then_inc(prob_kept, 1)

            def root(g):
                at_least(pool, var_kept, g + 1)
                at_least(pool, diag_kept, g)
                nc.gpsimd.tensor_tensor(rstdA[:], varA[:], power[0:S, :], ALU.pow).then_inc(rstd_kept, 1)

            def low_xn(g, q):
                at_least(pool, xnh_kept, g + 1)
                at_least(pool, z_done, H * g)
                nc.gpsimd.tensor_tensor(xn_l[:], xnT[:, q], xn_h[:].bitcast(F32), ALU.subtract).then_inc(xnl_kept, 1)

            root(0)
            low_xn(0, 0)

            def step(g, k, i, q):
                if k == 2 and exists(g + 1):
                    root(g + 1)
                if k == 3 and exists(g + 1):
                    low_xn(g + 1, 1 - q)
                if exists(g):
                    scale_prob(g, k)
                if isinstance(g, int) and g == 0 and k == 3:
                    pool.wait_ge(pair_kept, 2)
                    pool.wait_ge(split_lt, 2)
                    pool.dma_start(raw, w1.rearrange("e d f -> d e f")).then_inc(ws_1, 16)
                if isinstance(g, int) and g == 1:
                    low_w(raw[:, k * FF:(k + 1) * FF], w1_h[:, k * FF:(k + 1) * FF], w1_l[:, k * FF:(k + 1) * FF], k)

            steps_first(pool, step)

            first_part_computed(pool)
            pool.dma_start(w2raw[:, :, 1], w2.rearrange("e (c p) d -> p (e c) d", p=P)).then_inc(ws_2, 16)
            first_part_over(pool)
            laid = [0]

            def lay(ins):
                laid[0] += 1
                ins.then_inc(goal_kept, 1)
                pool.wait_ge(goal_kept, laid[0])

            lay(pool.iota(base[:], pattern=[[ROOM, NE]], base=0, channel_multiplier=0,
                          allow_small_or_imprecise_dtypes=True))
            lay(pool.iota(ebase[:], pattern=[[ROOM, NE]], base=0, channel_multiplier=0,
                          allow_small_or_imprecise_dtypes=True))
            lay(pool.iota(goal[:], pattern=[[-T, 2], [P, RT]], base=T, channel_multiplier=1,
                          allow_small_or_imprecise_dtypes=True))
            lay(pool.iota(starts[:], pattern=[[0, 1]], base=0, channel_multiplier=P,
                          allow_small_or_imprecise_dtypes=True))
            lay(pool.iota(tile_no[:], pattern=[[HT, 2]], base=0, channel_multiplier=1,
                          allow_small_or_imprecise_dtypes=True))
            lay(pool.memset(trow[:, :, :, :, D:ROWW], 0.0))
            lay(pool.memset(blank[:], 0.0))
            lay(pool.memset(spare_rows, 0.0))
            lay(pool.iota(blank[:, :, D:D + 1].bitcast(I32), pattern=[[P, NE]], base=2 * T, channel_multiplier=1))
            lay(pool.iota(spare_rows[:, :, D:D + 1].bitcast(I32), pattern=[[P, SPARE]], base=2 * T + NE * P,
                          channel_multiplier=1))
            LAID = laid[0]
            assert LAID == SETUP
            for k in range(SPARE):
                row = NE * ROOM + k * P
                pool.dma_start(sorted_dram[row:row + P, :], spare_rows[:, k]).then_inc(spares_in, 16)

            def root2(c, q):
                at_least(pool, var2_kept, c + 1)
                at_least(pool, trow_kept, c - 1)
                at_least(pool, mask_kept, c - 1)
                nc.gpsimd.tensor_tensor(rstdB[:, q], varB[:], power[:], ALU.pow).then_inc(rstd2_kept, 1)

            def set_goals(c, q):
                pool_waits((scattered[q], 16 * 2 * RT * (c // 2) if isinstance(c, int) else 8 * 2 * RT * (c - q)))
                nc.gpsimd.tensor_copy(trow[:, q, :, :, D:D + 1].bitcast(I32), goal[:].unsqueeze(3)).then_inc(goal_kept, 1)
                pool_waits((goal_kept, LAID + 2 * c + 1))
                nc.gpsimd.tensor_scalar(goal[:], goal[:], float(CT), None, ALU.add).then_inc(goal_kept, 1)

            def scatter(c, q, choice):
                if choice == 0:
                    pool_waits((goal_kept, LAID + 2 * c + 2), (trow_kept, c + 1), (posi_kept, c + 1))
                for r in range(RT):
                    pool.indirect_dma_start(
                        out=sorted_dram, out_offset=bass.IndirectOffsetOnAxis(ap=posi[:, q, choice, r:r + 1], axis=0),
                        in_=trow[:, q, choice, r], in_offset=None).then_inc(scattered[q], 16)

            def chunk(c, i, q, more):
                after_first = not isinstance(c, int) or c > 0
                root2(c, q)
                if after_first:
                    for choice in (0, 1):
                        scatter(c - 1, 1 - q, choice)
                set_goals(c, q)
                if isinstance(c, int) and c in (1, 2):
                    for e in range(4 * c - 4, 4 * c):
                        a = slice(FC * e, FC * e + FC)
                        low_w(w2raw[:, a, 1], w2s[:, a, 0], w2s[:, a, 1], NE + e)

            steps_second(pool, chunk)
            for choice in (0, 1):
                scatter(NCH - 1, (NCH - 1) % 2, choice)
            def tile(n, i, q):
                if is_tile(n):
                    pool_waits((tile_in[q], 16 * (i + 1)),
                               (y_out[q % 4], 16 * (2 * (i - 1) + q // 4 + 1)))
                    nc.gpsimd.tensor_copy(goals[:, q:q + 1], tin[:, q, D:D + 1].bitcast(I32)).then_inc(goal_read, 1)
                m = n - LAG_Y - 1
                if is_tile(m):
                    qm = (q - LAG_Y - 1) % RING
                    pool_waits((goal_read, m + 1),
                               (y_kept, m + 1))
                    pool.indirect_dma_start(out=y_dram, out_offset=bass.IndirectOffsetOnAxis(ap=goals[:, qm:qm + 1], axis=0),
                                            in_=ytok[:, qm % 4], in_offset=None).then_inc(y_out[qm % 4], 16)

            tiles(pool, tile)

            def add_first(c, i, q):
                at_least(pool, scaled, c + 1)
                at_least(pool, sum1_kept, c + 1)
                nc.gpsimd.tensor_tensor(osb[:, q], osb[:, q], yin[:, q, 1], ALU.add).then_inc(sum2_kept, 1)

            blocks(pool, NCH, FIN, add_first)

        @block.scalar
        def _(act):
            A = nc.scalar.activation
            act.dma_start(tokb[:], tok_b.rearrange("(d o) -> d o", o=1)).then_inc(ws_small, 16)
            act.dma_start(raw[:, 0:H * E], wq.rearrange("h d e -> d h e")).then_inc(ws_qk, 16)
            act.dma_start(raw[:, H * E:2 * H * E], wk.rearrange("h d e -> d h e")).then_inc(ws_qk, 16)
            act.dma_start(wrs[:], wr).then_inc(ws_small, 16)
            act.dma_start(brs[:], br.partition_broadcast(P)).then_inc(ws_small, 16)
            act.dma_start(b2raw[:], b2.rearrange("(o e) d -> o (e d)", o=1)).then_inc(ws_small, 16)
            act.dma_start(raw[:, 2 * H * E:2 * H * E + AC * D], wlt.rearrange("(c p) d -> p c d", p=P)).then_inc(ws_lt, 16)
            act.wait_ge(cs, 9)

            def keep_xT(g, c):
                at_least(act, xT_done, KC * g + c + 1)
                at_least(act, h_done, g)
                A(xT[:, c], front_ps[c][:, 0:GB * NROW].rearrange("p (b r) -> p b r", b=GB), ACT.Copy).then_inc(xT_kept, 1)

            def keep_h(g):
                at_least(act, h_done, g + 1)
                at_least(act, hc_done, g)
                at_least(act, h_out, 16 * g)
                A(hT[:], front_ps[0][:, 0:GT], ACT.Identity, bias=tokb[:]).then_inc(h_kept, 1)

            def keep_sq(g):
                at_least(act, hc_done, g + 1)
                at_least(act, var_done, g)
                A(sqA[:], front_ps[1][:, 0:GT], ACT.Square).then_inc(sq_kept, 1)

            def keep_hc(g):
                at_least(act, xnT_kept, g)
                A(hcA[:], front_ps[1][:, 0:GT], ACT.Copy).then_inc(hcs_kept, 1)

            def keep_xnh(g, q):
                at_least(act, xnT_kept, g + 1)
                at_least(act, z_done, H * g)
                at_least(act, xnl_kept, g)
                A(xn_h[:], xnT[:, q], ACT.Copy).then_inc(xnh_kept, 1)

            def keep_xtokh(g, q):
                at_least(act, xn_done, g + 1)
                at_least(act, mix_done, UN * (g - 1))
                A(xtok_h[:, q], front_ps[1][0:S, :].rearrange("t (b d) -> t b d", b=GB), ACT.Copy).then_inc(xtokh_kept, 1)

            def keep_z(g, h, q):
                at_least(act, z_done, H * g + h + 1)
                at_least(act, score_done, UN * (g - 1))
                A(z[:, q, :, h, :], front_ps[h % 2][:, 0:GT].rearrange("d (b j) -> d b j", b=GB),
                  ACT.Copy).then_inc(z_kept, 1)

            for c in range(KC):
                keep_xT(0, c)
            act.wait_ge(ws_small, 4 * 16)
            keep_h(0)
            keep_sq(0)
            keep_hc(0)
            keep_xnh(0, 0)
            keep_xtokh(0, 0)
            for h in range(H):
                keep_z(0, h, 0)

            def step(g, k, i, q):
                more = exists(g + 1)
                gt, kt = back(g, k, LAG_TK)
                if exists(gt):
                    n = UN * gt + kt
                    at_least(act, probT_done, n + 1)
                    at_least(act, mix_done, n - 1)
                    A(probT_h[:, kt % 2], probT_ps[kt % 2][0:S, 0:GT].rearrange("j (h i) -> j h i", h=HH),
                      ACT.Copy).then_inc(probTh_kept, 1)
                if more:
                    if k == 0:
                        keep_xT(g + 1, 0)
                    if k == 4:
                        keep_xtokh(g + 1, 1 - q)
                    for h in Z_FIRST.get(k, ()):
                        keep_z(g + 1, h, 1 - q)
                def exponentials():
                    if exists(g):
                        n = UN * g + k
                        at_least(act, cent_kept, n + 1)
                        at_least(act, prob_kept, n - 1)
                        A(expo[:, k % 2], cent[:, k % 2], ACT.Exp, scale=1.0 / E).then_inc(exp_kept, 1)

                def keep_mix():
                    gm, km = back(g, k, LAG_M)
                    if exists(gm):
                        n = UN * gm + km
                        half, b = km // GB, km % GB
                        at_least(act, mix_done, n + 1)
                        at_least(act, val_done, H * gm + HH * half - HH)
                        A(mix_h[:, half * HH:(half + 1) * HH, b, :],
                          mix_ps[:, 0:GT].rearrange("d (h i) -> d h i", h=HH), ACT.Copy).then_inc(mixh_kept, 1)

                if k == 1:
                    exponentials()
                if more:
                    if k == 0:
                        keep_xT(g + 1, 1)
                    if k == 1:
                        keep_h(g + 1)
                keep_mix()
                if k != 1:
                    exponentials()
                gv, h = back(g, k, LAG_V)
                if exists(gv):
                    a = H * gv + h
                    half = h // HH
                    at_least(act, val_done, a + 1)
                    if h % HH == 0:
                        at_least(act, val_out[half], 16 * gv)
                    A(val[:, half, :, h % HH, :], val_ps[:, 0:GT].rearrange("f (b i) -> f b i", b=GB),
                      ACT.Copy).then_inc(val_kept, 1)
                if more:
                    if k == 1:
                        keep_sq(g + 1)
                        keep_hc(g + 1)
                    for h in Z_THEN.get(k, ()):
                        keep_z(g + 1, h, 1 - q)
                if k == 3 and more:
                    keep_xnh(g + 1, 1 - q)
                if isinstance(g, int) and g == 0 and k == 3:
                    act.wait_ge(split_b2, 2)
                    act.dma_start(b2s[1:2, :].bitcast(F32), b2_l[:].bitcast(F32)).then_inc(b2_moved, 16)
                if isinstance(g, int) and g == 1:
                    act.wait_ge(ws_1, 16)
                    A(w1_h[:, k * FF:(k + 1) * FF], raw[:, k * FF:(k + 1) * FF], ACT.Copy).then_inc(high_kept, 1)

            steps_first(act, step)

            first_part_computed(act)

            def keep_aTh(c, j):
                m = AC * c + j
                at_least(act, aT_done, m + 1)
                at_least(act, proj_done, m - TURNS + 1)
                A(aT_h[:, j % TURNS], turn_ps[j % TURNS][:], ACT.Copy).then_inc(aTh_kept, 1)

            def keep_sq2(c):
                at_least(act, hc2_done, c + 1)
                at_least(act, var2_done, c)
                A(sqB[:], hc_ps[:], ACT.Square).then_inc(sq2_kept, 1)
                at_least(act, tok_done, c)
                A(hcB[:], hc_ps[:], ACT.Copy).then_inc(hcs2_kept, 1)

            def keep_trow(c, q):
                at_least(act, tok_done, c + 1)
                at_least(act, rstd2_kept, c + 1)
                at_least(act, scattered[q], 16 * 2 * RT * (c // 2) if isinstance(c, int) else 8 * 2 * RT * (c - q))
                act.wait_ge(goal_kept, SETUP)
                for r in range(RT):
                    ins = A(trow[:, q, :, r, 0:D], tok_ps[:, r * D:(r + 1) * D].unsqueeze(1).to_broadcast([P, 2, D]),
                            ACT.Copy, scale=rstdB[:, q, r:r + 1])
                ins.then_inc(trow_kept, 1)

            def keep_res(c):
                at_least(act, res_done, c + 1)
                if isinstance(c, int) and c >= NCH - 3:
                    act.wait_ge(spares_in, 16 * SPARE)
                dst = h1tok[:, c * RT:(c + 1) * RT] if isinstance(c, int) else h1tok[:, bass.ds(c * RT, RT)]
                A(dst, res_ps[:].rearrange("p (r d) -> p r d", r=RT), ACT.Copy).then_inc(res_kept, 1)

            def keep_gapexp(c):
                at_least(act, gap_kept, c + 1)
                A(top[:, 3], top[:, 2], ACT.Exp).then_inc(gapexp_kept, 1)

            for j in range(AC):
                keep_aTh(0, j)

            def chunk(c, i, q, more):
                for j in range(AC):
                    if more:
                        keep_aTh(c + 1, j)
                    if j == 1:
                        keep_sq2(c)
                    if j == 3:
                        keep_res(c)
                    if j == AC - 1:
                        keep_trow(c, q)
                        keep_gapexp(c)
                    if isinstance(c, int) and c in (1, 2) and j >= AC - 4:
                        act.wait_ge(ws_2, 16)
                        a = slice(FC * (4 * c + j - AC), FC * (4 * c + j - AC) + FC)
                        A(w2s[:, a, 0], w2raw[:, a, 1], ACT.Copy).then_inc(high_kept, 1)

            steps_second(act, chunk)
            lay_pads(act, range(1, NE, 2))

            def tile(n, i, q):
                if is_tile(n):
                    at_least(act, xt_done, n + 1)
                    at_least(act, hid_done, n - 1)
                    A(x_h[:, q % 2], xt_ps[:, 0:P], ACT.Copy).then_inc(xh_kept, 1)
                m = n - LAG_R
                if is_tile(m):
                    at_least(act, back_done, m + 1)
                    at_least(act, y_done, m - 1)
                    A(hid_h[:, (q - LAG_R) % 2], back_ps[(q - LAG_R) % 2][:], ACT.Relu).then_inc(hidh_kept, 1)
            tiles(act, tile)

            def weigh_first(c, i, q):
                at_least(act, y_in[q], 32 * (i + 1))
                for r in range(RT):
                    ins = A(yin[:, q, 1, r], yin[:, q, 1, r], ACT.Copy, scale=weight_of(1, c, r))
                ins.then_inc(scaled, 1)

            def send(c, q):
                at_least(act, sum2_kept, c + 1)
                sl = slice(c * CT, (c + 1) * CT) if isinstance(c, int) else bass.ds(c * CT, CT)
                act.dma_start(out[sl, :].rearrange("(r p) d -> p r d", p=P), osb[:, q]).then_inc(out_sent[q], 16)

            def weigh_and_send(c, i, q):
                weigh_first(c, i, q)
                if not isinstance(c, int) or c > 0:
                    send(c - 1, (q - 1) % FIN)

            act.wait_ge(route, NR * NCH)
            blocks(act, NCH, FIN, weigh_and_send)
            send(NCH - 1, (NCH - 1) % FIN)
            for q in range(FIN):
                act.wait_ge(out_sent[q], 16 * ((NCH - q + FIN - 1) // FIN))

        @block.vector
        def _(dve):
            V = nc.vector
            dve.wait_ge(cs, 9)
            for j in range(4):
                dve.wait_ge(qkT_done, j + 1)
                V.tensor_copy(raw[0:E, 2048 + 512 * j:2048 + 512 * (j + 1)], bank[2 + j][0:E, :]).then_inc(qkT_kept, 1)
            def split_pair(j):
                dve.wait_ge(pair_done, j + 1)
                src = bank[6 + j][:].rearrange("p (h d) -> p h d", h=4)
                V.tensor_copy(pair_h[:, 4 * j:4 * j + 4], src).then_inc(qkT_kept, 1)
                dve.wait_ge(qkT_kept, 5 + j)
                V.tensor_tensor(pair_l[:, 4 * j:4 * j + 4], src, pair_h[:, 4 * j:4 * j + 4].bitcast(F32),
                                ALU.subtract).then_inc(pair_kept, 1)

            def keep_var(g):
                at_least(dve, var_done, g + 1)
                at_least(dve, rstd_kept, g)
                V.tensor_scalar(varA[:], front_ps[0][0:S, 0:GB], EPS, None, ALU.add).then_inc(var_kept, 1)

            def keep_diag(g):
                at_least(dve, rstd_kept, g + 1)
                at_least(dve, spread_done, g)
                V.tensor_tensor(diag[:], ident[0:S, 0:S].unsqueeze(1).to_broadcast([S, GB, S]),
                                rstdA[:].unsqueeze(2).to_broadcast([S, GB, S]), ALU.mult).then_inc(diag_kept, 1)

            def keep_xnT(g, q):
                at_least(dve, spread_done, g + 1)
                at_least(dve, hcs_kept, g + 1)
                at_least(dve, score_done, UN * (g - 1))
                V.tensor_tensor(xnT[:, q], front_ps[0][:, 0:GT], hcA[:], ALU.mult).then_inc(xnT_kept, 1)

            def keep_xtokl(g, q):
                at_least(dve, xtokh_kept, g + 1)
                at_least(dve, mix_done, UN * (g - 1))
                V.tensor_tensor(xtok_l[:, q], front_ps[1][0:S, :].rearrange("t (b d) -> t b d", b=GB),
                                xtok_h[:, q].bitcast(F32), ALU.subtract).then_inc(xtokl_kept, 1)

            keep_var(0)
            split_pair(0)
            keep_diag(0)
            split_pair(1)
            keep_xnT(0, 0)
            keep_xtokl(0, 0)

            dve.wait_ge(ws_v, 16)
            V.tensor_copy(wv_h[:], wv_raw).then_inc(split_v, 1)
            dve.wait_ge(split_v, 1)
            V.tensor_tensor(wv_l[:], wv_raw, wv_h[:].bitcast(F32), ALU.subtract).then_inc(split_v, 1)

            def split_rest(k):
                if k == 0:
                    dve.wait_ge(ws_small, 4 * 16)
                    V.tensor_copy(b2s[0:1, :], b2raw[:]).then_inc(split_b2, 1)
                    dve.wait_ge(split_b2, 1)
                    V.tensor_tensor(b2_l[:], b2raw[:], b2s[0:1, :].bitcast(F32), ALU.subtract).then_inc(split_b2, 1)
                    V.tensor_copy(ones2[:], ones[0:2, :]).then_inc(split_b2, 1)
                    V.tensor_copy(ones_r[:], ones[:]).then_inc(split_b2, 1)
                    V.tensor_copy(before_r[:], before[:]).then_inc(split_b2, 1)
                if k == 1:
                    dve.wait_ge(ws_lt, 16)
                    lt = raw[:, 2 * H * E:2 * H * E + AC * D].rearrange("p (c d) -> p c d", c=AC)
                    V.tensor_copy(wlt_h[:], lt).then_inc(split_lt, 1)
                    dve.wait_ge(split_lt, 1)
                    V.tensor_tensor(wlt_l[:], lt, wlt_h[:].bitcast(F32), ALU.subtract).then_inc(split_lt, 1)

            def step(g, k, i, q):
                gs, ks = back(g, k, LAG_S)
                if exists(gs):
                    n = UN * gs + ks
                    at_least(dve, exp_kept, n + 1)
                    V.tensor_reduce(total[:, ks % 2], expo[:, ks % 2], AX_X, ALU.add).then_inc(total_kept, 1)
                sc = score_ps[k % 2][0:S, 0:GT].rearrange("i (h j) -> i h j", h=HH)
                if exists(g):
                    n = UN * g + k
                    at_least(dve, score_done, n + 1)
                    V.tensor_reduce(peak[:, k % 2], sc, AX_X, ALU.max).then_inc(peak_kept, 1)
                if exists(gs):
                    n = UN * gs + ks
                    at_least(dve, total_kept, n + 1)
                    at_least(dve, prob_kept, n - 1)
                    V.reciprocal(inv[:, ks % 2], total[:, ks % 2]).then_inc(inv_kept, 1)
                if exists(g):
                    n = UN * g + k
                    at_least(dve, peak_kept, n + 1)
                    at_least(dve, exp_kept, n - 1)
                    V.tensor_tensor(cent[:, k % 2], sc, peak[:, k % 2].unsqueeze(2).to_broadcast([S, HH, S]),
                                    ALU.subtract).then_inc(cent_kept, 1)
                if k == 2 and exists(g + 1):
                    keep_var(g + 1)
                gt, kt = back(g, k, LAG_TK)
                if exists(gt):
                    n = UN * gt + kt
                    at_least(dve, probTh_kept, n + 1)
                    V.tensor_tensor(probT_l[:, kt % 2], probT_ps[kt % 2][0:S, 0:GT].rearrange("j (h i) -> j h i", h=HH),
                                    probT_h[:, kt % 2].bitcast(F32), ALU.subtract).then_inc(probTl_kept, 1)
                if k == 3 and exists(g + 1):
                    keep_xnT(g + 1, 1 - q)
                if k == 4 and exists(g + 1):
                    keep_xtokl(g + 1, 1 - q)
                gm, km = back(g, k, LAG_M)
                if exists(gm):
                    n = UN * gm + km
                    half, b = km // GB, km % GB
                    at_least(dve, mixh_kept, n + 1)
                    V.tensor_tensor(mix_l[:, half * HH:(half + 1) * HH, b, :],
                                    mix_ps[:, 0:GT].rearrange("d (h i) -> d h i", h=HH),
                                    mix_h[:, half * HH:(half + 1) * HH, b, :].bitcast(F32),
                                    ALU.subtract).then_inc(mixl_kept, 1)
                if exists(g + 1):
                    if k == 2:
                        keep_diag(g + 1)

                if isinstance(g, int) and g == 0:
                    split_rest(k)

            steps_first(dve, step)

            first_part_computed(dve)

            def keep_aTl(c, j):
                at_least(dve, aTh_kept, AC * c + j + 1)
                at_least(dve, proj_done, AC * c + j - TURNS + 1)
                V.tensor_tensor(aT_l[:, j % TURNS], turn_ps[j % TURNS][:], aT_h[:, j % TURNS].bitcast(F32),
                                ALU.subtract).then_inc(aTl_kept, 1)

            def keep_h1(c, i, q):
                at_least(dve, proj_done, AC * (c + 1))
                if isinstance(c, int):
                    dve.wait_ge(a_in[q], 32 * (c // 2 + 1))
                else:
                    dve.wait_ge(a_in[q], 16 * (c - q + 2))
                at_least(dve, res_done, c - 1)
                V.tensor_tensor(h1[:, q], proj_ps[:], hch[q][:], ALU.add).then_inc(h1_kept, 1)

            def keep_var2(c):
                at_least(dve, var2_done, c + 1)
                at_least(dve, rstd2_kept, c)
                V.tensor_scalar(varB[:], var_ps, EPS, None, ALU.add).then_inc(var2_kept, 1)

            step_no = [0]
            wide = lambda a: a.unsqueeze(2).to_broadcast([P, RT, NE])

            def link(c, ins):
                step_no[0] += 1
                ins.then_inc(route, 1)
                dve.wait_ge(route, NR * c + step_no[0])

            def take_logits(c, q):
                step_no[0] = 0
                at_least(dve, lg_done, c + 1)
                at_least(dve, rstd2_kept, c + 1)
                link(c, V.tensor_tensor(lg[:], count_ps[:, 0:RT * NE].rearrange("p (r e) -> p r e", r=RT),
                                        wide(rstdB[:, q]), ALU.mult))
                link(c, V.tensor_tensor(lg[:], lg[:], brs[:].unsqueeze(1).to_broadcast([P, RT, NE]), ALU.add))

            def largest(c, which):
                m = top[:, which]
                link(c, V.tensor_reduce(m, lg[:], AX_X, ALU.max))
                link(c, V.tensor_tensor(eq[:], lg[:], wide(m), ALU.is_equal))

            def first_of_equals(c, which, one):
                kk = top[:, 4 + which]
                link(c, V.tensor_tensor(key[:], eq[:], rank[:], ALU.mult))
                link(c, V.tensor_reduce(kk, key[:], AX_X, ALU.max))
                link(c, V.tensor_tensor(one[:], rank[:], wide(kk), ALU.is_equal))

            def without_first(c):
                link(c, V.scalar_tensor_tensor(lg[:], one1[:], -3.0e38, lg[:], ALU.mult, ALU.add))

            def chosen(c):
                at_least(dve, count_done, c)
                V.tensor_tensor(mask[:], one1[:], one2[:], ALU.add).then_inc(mask_kept, 1)
                V.tensor_tensor(top[:, 2], top[:, 1], top[:, 0], ALU.subtract).then_inc(gap_kept, 1)

            def weigh(c):
                at_least(dve, gapexp_kept, c + 1)
                link(c, V.tensor_scalar(top[:, 6], top[:, 3], 1.0, None, ALU.add))
                link(c, V.reciprocal(top[:, 7], top[:, 6]))
                link(c, V.tensor_tensor(top[:, 6], top[:, 7], top[:, 3], ALU.mult))
                dst = wtab[:, :, c * RT:(c + 1) * RT] if isinstance(c, int) else wtab[:, :, bass.ds(c * RT, RT)]
                link(c, V.tensor_copy(dst, top[:, 6:8]))

            def rows_of(c, q):
                at_least(dve, count_done, c + 1)
                dve.wait_ge(goal_kept, SETUP)
                link(c, V.tensor_tensor(place[:], count_ps[:, 64:64 + RT * NE].rearrange("p (r e) -> p r e", r=RT),
                                        base[:].unsqueeze(1).to_broadcast([P, RT, NE]), ALU.add))
                link(c, V.tensor_tensor(base[:], count_ps[:, 128:128 + NE], base[:], ALU.add))
                link(c, V.tensor_tensor(one2[:], one2[:], place[:], ALU.mult))
                link(c, V.tensor_reduce(posf[:, 0], one2[:], AX_X, ALU.add))
                link(c, V.tensor_tensor(one1[:], one1[:], place[:], ALU.mult))
                link(c, V.tensor_reduce(posf[:, 1], one1[:], AX_X, ALU.add))
                at_least(dve, scattered[q], 16 * 2 * RT * (c // 2) if isinstance(c, int) else 8 * 2 * RT * (c - q))
                V.tensor_copy(posi[:, q], posf[:]).then_inc(posi_kept, 1)

            for j in range(AC):
                keep_aTl(0, j)

            CHOSEN = 13

            def chunk(c, i, q, more):
                after_first = not isinstance(c, int) or c > 0
                keep_h1(c, i, q)
                for j in range(AC):
                    if more:
                        keep_aTl(c + 1, j)
                    if j == 0 and after_first:
                        step_no[0] = CHOSEN
                        rows_of(c - 1, 1 - q)
                    if j == 3:
                        keep_var2(c)
                        if after_first:
                            weigh(c - 1)
                            assert step_no[0] == NR, step_no
                    if j == 4:
                        take_logits(c, q)
                        largest(c, 0)
                    if j == 5:
                        first_of_equals(c, 0, one1)
                        without_first(c)
                    if j == 6:
                        largest(c, 1)
                    if j == AC - 1:
                        first_of_equals(c, 1, one2)
                        chosen(c)
                        assert step_no[0] == CHOSEN, step_no

            steps_second(dve, chunk)
            step_no[0] = CHOSEN
            rows_of(NCH - 1, (NCH - 1) % 2)
            weigh(NCH - 1)

            done = [0]

            def then(ins):
                done[0] += 1
                ins.then_inc(route, 1)
                dve.wait_ge(route, NR * NCH + done[0])

            V.tensor_copy(padi[:], base[0:1, :]).then_inc(padi_kept, 1)
            then(V.tensor_tensor(held[:], base[:], ebase[:], ALU.subtract))
            V.tensor_scalar(holds[0:NT], held[0:NT], starts[0:NT, 0:1], None, ALU.is_gt).then_inc(holds_kept, 1)
            then(V.memset(whosei[:], 0))
            dve.wait_ge(counted, 1)
            then(V.tensor_tensor(past[:], tile_no[:].unsqueeze(2).to_broadcast([HT, 2, NE]),
                                 cum_ps[0:HT].unsqueeze(1).to_broadcast([HT, 2, NE]), ALU.is_ge))
            then(V.tensor_scalar(jump[:], ntile_ps, -float(P), float(ROOM), ALU.mult, ALU.add))
            then(V.tensor_reduce(ahead[:], past[:], AX_X, ALU.add))
            then(V.tensor_scalar(entry[:, 0], ahead[:], float(NE - 1), None, ALU.min))
            then(V.tensor_tensor(jumps[:], past[:], jump[0:HT].unsqueeze(1).to_broadcast([HT, 2, NE]), ALU.mult))
            then(V.tensor_reduce(ahead[:], jumps[:], AX_X, ALU.add))
            V.scalar_tensor_tensor(entry[:, 1], tile_no[:], float(P), ahead[:], ALU.mult, ALU.add).then_inc(entries_kept, 1)
            dve.wait_ge(listed, 1)
            then(V.tensor_copy(whosei[:, 4:4 + TILES], row_ps[:, 0:TILES]))
            V.tensor_copy(wherei[:], row_ps[:, TILES:2 * TILES]).then_inc(table, 1)

            dve.wait_ge(table, 1)
            dve.wait_ge(b1_in, 16)

            experts = {}

            def tile(n, i, q):
                if q == 0:
                    experts["now"] = tile_experts(dve, i)
                if is_tile(n):
                    at_least(dve, xh_kept, n + 1)
                    at_least(dve, hid_done, n - 1)
                    V.tensor_tensor(x_l[:, q % 2], xt_ps[:, 0:P], x_h[:, q % 2].bitcast(F32), ALU.subtract).then_inc(xl_kept, 1)
                m = n - LAG_H
                if is_tile(m):
                    qm = (q - LAG_H) % RING
                    at_least(dve, hid_done, m + 1)
                    at_least(dve, back_done, m - 1)
                    e = experts["now"][4 + q - LAG_H]
                    V.tensor_tensor(pre[:, qm % 2], hid_ps[qm % 2][:], b1b[:, bass.ds(e * FF, FF)], ALU.add).then_inc(pre_kept, 1)
                m = n - LAG_R
                if is_tile(m):
                    qm = (q - LAG_R) % RING
                    at_least(dve, hidh_kept, m + 1)
                    at_least(dve, y_done, m - 1)
                    V.scalar_tensor_tensor(hid_l[:, qm % 2], back_ps[qm % 2][:], 0.0, hid_h[:, qm % 2].bitcast(F32),
                                           ALU.max, ALU.subtract).then_inc(hidl_kept, 1)
                m = n - LAG_Y
                if is_tile(m):
                    qm = (q - LAG_Y) % RING
                    at_least(dve, y_done, m + 1)
                    if isinstance(m, int):
                        at_least(dve, y_out[qm % 4], 16 * (m // 4))
                    else:
                        dve.wait_ge(y_out[qm % 4], 4 * (m - qm % 4))
                    V.tensor_reduce(ytok[:, qm % 4], y_ps[qm % 2][:, 0:2 * D].rearrange("p (h d) -> p d h", h=2),
                                    AX_X, ALU.add).then_inc(y_kept, 1)

            tiles(dve, tile)

            def total_of(c, i, q):
                at_least(dve, y_in[q], 32 * (i + 1))
                at_least(dve, out_sent[q], 16 * i)
                for r in range(RT):
                    w, res = weight_of(0, c, r), h1tok[:, c * RT + r] if isinstance(c, int) else \
                        h1tok[:, bass.ds(c * RT + r, 1)].rearrange("p o d -> p (o d)")
                    ins = V.scalar_tensor_tensor(osb[:, q, r], yin[:, q, 0, r], w, res, ALU.mult, ALU.add)
                ins.then_inc(sum1_kept, 1)

            dve.wait_ge(res_kept, NCH)
            blocks(dve, NCH, FIN, total_of)

        @block.tensor
        def _(pe):
            pe.wait_ge(cs, 9)
            def turn_x(g, c, i, q):
                at_least(pe, z_kept, H * g - 1 + c)
                if c == 0:
                    at_least(pe, x_in[q], 16 * (i + 1))
                for b in range(GB):
                    ins = nc.tensor.transpose(front_ps[c][:, b * NROW:(b + 1) * NROW],
                                              xin[:, q, b, c * P:(c + 1) * P], ident[0:NROW, 0:NROW])
                ins.then_inc(xT_done, 1)

            def embed(g):
                n = 0
                for c in range(KC):
                    at_least(pe, xT_kept, KC * g + c + 1)
                    for late in (0, 1):
                        ins = mm(front_ps[0][:, 0:GT], tokw[:, late * KC + c], xT[:, c, :, late:late + S],
                                 start=(n == 0), stop=(n == 2 * KC - 1))
                        n += 1
                ins.then_inc(h_done, 1)

            def centre(g):
                at_least(pe, h_kept, g + 1)
                mm(front_ps[1][:, 0:GT], center[:], hT[:], start=True, stop=True).then_inc(hc_done, 1)

            def variance(g):
                at_least(pe, sq_kept, g + 1)
                for b in range(GB):
                    ins = mm(front_ps[0][0:S, b:b + 1], sqA[:, b * S:(b + 1) * S], average[:, 0:1], start=True, stop=True)
                ins.then_inc(var_done, 1)

            def spread(g):
                at_least(pe, diag_kept, g + 1)
                mm(front_ps[0][:, 0:GT], ones[0:S, :], diag[:], start=True, stop=True).then_inc(spread_done, 1)

            def turn_xn(g, q):
                at_least(pe, xnT_kept, g + 1)
                for b in range(GB):
                    ins = nc.tensor.transpose(front_ps[1][0:S, b * D:(b + 1) * D], xnT[:, q, b * S:(b + 1) * S], ident[:])
                ins.then_inc(xn_done, 1)

            def make_z(g, h):
                if h == 0:
                    at_least(pe, xnh_kept, g + 1)
                    at_least(pe, xnl_kept, g + 1)
                if h == 1:
                    at_least(pe, xtokl_kept, g + 1)
                if h >= 2:
                    at_least(pe, z_kept, H * g + h - 1)
                three(front_ps[h % 2][:, 0:GT], pair_h[:, h], pair_l[:, h], xn_h[:], xn_l[:],
                      True, True).then_inc(z_done, 1)

            for c in range(KC):
                turn_x(0, c, 0, 0)
            pe.wait_ge(ws_tok, 16)
            embed(0)
            pe.wait_ge(ws_qk, 32)
            for j in range(4):
                for m in range(4):
                    o = (4 * j + m) * E
                    ins = nc.tensor.transpose(bank[2 + j][0:E, m * D:(m + 1) * D], raw[:, o:o + E], ident[:])
                ins.then_inc(qkT_done, 1)
            centre(0)
            variance(0)
            pe.wait_ge(qkT_kept, 4)
            for j in range(2):
                for m in range(4):
                    h = 4 * j + m
                    qT = raw[0:E, 2048 + h * D:2048 + (h + 1) * D]
                    kT = raw[0:E, 2048 + (H + h) * D:2048 + (H + h + 1) * D]
                    ins = mm(bank[6 + j][:, m * D:(m + 1) * D], qT, kT, start=True, stop=True)
                ins.then_inc(pair_done, 1)
            spread(0)
            turn_xn(0, 0)
            pe.wait_ge(pair_kept, 2)
            for h in range(H):
                make_z(0, h)

            def step(g, k, i, q):
                more = exists(g + 1)
                if exists(g):
                    n = UN * g + k
                    half, b = k // GB, k % GB
                    at_least(pe, z_kept, H * g + (half + 1) * HH)
                    at_least(pe, cent_kept, n - 1)
                    mm(score_ps[k % 2][0:S, 0:GT], xnT[:, q, b * S:(b + 1) * S], z[:, q, b, half * HH:(half + 1) * HH, :],
                       start=True, stop=True).then_inc(score_done, 1)
                if more:
                    if k == 0:
                        turn_x(g + 1, 0, i + q, 1 - q)
                    if k == 1:
                        embed(g + 1)
                    if k == 4:
                        turn_xn(g + 1, 1 - q)
                    for h in Z_FIRST.get(k, ()):
                        make_z(g + 1, h)
                gm, km = back(g, k, LAG_M)
                if exists(gm):
                    n = UN * gm + km
                    qm = q if k >= LAG_M else 1 - q
                    at_least(pe, probTl_kept, n + 1)
                    at_least(pe, xtokl_kept, gm + 1)
                    at_least(pe, mixl_kept, n)
                    three(mix_ps[:, 0:GT], xtok_h[:, qm, km % GB], xtok_l[:, qm, km % GB],
                          probT_h[:, km % 2], probT_l[:, km % 2], True, True).then_inc(mix_done, 1)
                if more and k == 2:
                    variance(g + 1)
                gt, kt = back(g, k, LAG_T)
                if exists(gt):
                    n = UN * gt + kt
                    at_least(pe, prob_kept, n + 1)
                    at_least(pe, probTl_kept, n - 1)
                    for m in range(HH):
                        ins = nc.tensor.transpose(probT_ps[kt % 2][0:S, m * S:(m + 1) * S], prob[:, kt % 2, m], ident[0:S, 0:S])
                    ins.then_inc(probT_done, 1)
                if more and k == 3:
                    spread(g + 1)
                gv, h = back(g, k, LAG_V)
                if exists(gv):
                    at_least(pe, mixl_kept, UN * gv + (h // HH + 1) * GB)
                    at_least(pe, val_kept, H * gv + h)
                    three(val_ps[:, 0:GT], wv_h[:, h], wv_l[:, h], mix_h[:, h], mix_l[:, h], True, True).then_inc(val_done, 1)
                if more:
                    if k == 0:
                        turn_x(g + 1, 1, i + q, 1 - q)
                    if k == 1:
                        centre(g + 1)
                    for h in Z_THEN.get(k, ()):
                        make_z(g + 1, h)

            pe.wait_ge(split_v, 2)
            steps_first(pe, step)

            first_part_computed(pe)
            pe.wait_ge(split_lt, 2)
            pe.wait_ge(split_b2, 5)
            pe.wait_ge(b2_moved, 16)

            def turn_a(c, j, q):
                m = AC * c + j
                if j == 0:
                    if isinstance(c, int):
                        pe.wait_ge(a_in[q], 32 * (c // 2 + 1))
                    else:
                        pe.wait_ge(a_in[q], 16 * (c - q + 2))
                at_least(pe, aTl_kept, m - TURNS + 1)
                for r in range(RT):
                    ins = nc.tensor.transpose(turn_ps[j % TURNS][:, r * P:(r + 1) * P], arow[q][:, r, j * P:(j + 1) * P], ident[:])
                ins.then_inc(aT_done, 1)

            def project(c, j):
                m = AC * c + j
                if j == 0:
                    at_least(pe, h1_kept, c)
                at_least(pe, aTh_kept, m + 1)
                at_least(pe, aTl_kept, m + 1)
                three(proj_ps[:], wlt_h[:, j], wlt_l[:, j], aT_h[:, j % TURNS], aT_l[:, j % TURNS],
                      j == 0, j == AC - 1).then_inc(proj_done, 1)

            def centre2(c, q):
                at_least(pe, h1_kept, c + 1)
                at_least(pe, hcs2_kept, c)
                mm(hc_ps[:], center[:], h1[:, q], start=True, stop=True).then_inc(hc2_done, 1)

            def variance2(c):
                at_least(pe, sq2_kept, c + 1)
                at_least(pe, posi_kept, c)
                for r in range(RT):
                    ins = mm(var_ps[:, r:r + 1], sqB[:, r * P:(r + 1) * P], average[:, 0:1], start=True, stop=True)
                ins.then_inc(var2_done, 1)

            def logits(c):
                at_least(pe, hcs2_kept, c + 1)
                at_least(pe, var2_kept, c + 1)
                for r in range(RT):
                    ins = mm(count_ps[:, r * NE:(r + 1) * NE], hcB[:, r * P:(r + 1) * P], wrs[:], start=True, stop=True)
                ins.then_inc(lg_done, 1)

            def turn_tok(c):
                at_least(pe, res_kept, c + 1)
                for r in range(RT):
                    ins = nc.tensor.transpose(tok_ps[:, r * D:(r + 1) * D], hcB[:, r * P:(r + 1) * P], ident[:])
                ins.then_inc(tok_done, 1)

            def turn_res(c, q):
                at_least(pe, trow_kept, c)
                for r in range(RT):
                    ins = nc.tensor.transpose(res_ps[:, r * D:(r + 1) * D], h1[:, q, r * P:(r + 1) * P], ident[:])
                ins.then_inc(res_done, 1)

            def count(c):
                at_least(pe, mask_kept, c + 1)
                m2 = mask[:].rearrange("p r e -> p (r e)")
                for back_by in range(RT):
                    n = (RT - back_by) * NE
                    mm(count_ps[:, 64 + back_by * NE:64 + RT * NE], before_r[:] if back_by == 0 else ones_r[:], m2[:, 0:n],
                       start=back_by == 0, stop=back_by == RT - 1)
                for r in range(RT):
                    ins = mm(count_ps[:, 128:128 + NE], ones_r[:], mask[:, r], start=r == 0, stop=r == RT - 1)
                ins.then_inc(count_done, 1)

            for j in range(AC + LAG_P):
                if j < AC:
                    turn_a(0, j, 0)
                if j >= LAG_P:
                    project(0, j - LAG_P)

            def chunk(c, i, q, more):
                for j in range(AC + LAG_P):
                    if more and j < AC:
                        turn_a(c + 1, j, 1 - q)
                    if j == 0 and (not isinstance(c, int) or c > 0):
                        count(c - 1)
                    if j == 1:
                        centre2(c, q)
                    if j == 3:
                        variance2(c)
                    if j == 4:
                        logits(c)
                    if j == 5:
                        turn_tok(c)
                    if more and j >= LAG_P:
                        project(c + 1, j - LAG_P)
                    if j == 2:
                        turn_res(c, q)

            steps_second(pe, chunk)
            count(NCH - 1)

            pe.wait_ge(holds_kept, 1)
            pe.wait_ge(trow_kept, NCH)
            for k in range(NE):
                mm(cum_ps[:, k:NE], ones[0:NT, :], holds[0:NT, 0:NE - k], start=k == 0, stop=k == NE - 1)
            mm(ntile_ps, ones[0:NT, :], holds[0:NT, :], start=True, stop=True).then_inc(counted, 1)
            pe.wait_ge(entries_kept, 1)
            for which in (0, 1):
                for half in (0, 1):
                    at = (2 * which + half) * HT
                    ins = mm(row_ps[:, at:at + HT], entry[:, which, half:half + 1], ident[0:HT, 0:HT], start=True, stop=True)
            ins.then_inc(listed, 1)
            pe.wait_ge(table, 1)
            pe.wait_ge(low_kept, 2 * NE)
            pe.wait_ge(posi_kept, NCH)
            pe.wait_ge(trow_kept, NCH)
            pe.wait_ge(res_kept, NCH)

            experts = {}

            def tile(n, i, q):
                if q == 0:
                    experts["now"] = tile_experts(pe, i)
                if is_tile(n):
                    at_least(pe, tile_in[q], 16 * (i + 1))
                    at_least(pe, xl_kept, n)
                    nc.tensor.transpose(xt_ps[:, 0:P], tin[:, q, 0:D], ident[:]).then_inc(xt_done, 1)
                m = n - LAG_H
                if is_tile(m):
                    b = (q - LAG_H) % 2
                    e = experts["now"][4 + q - LAG_H]
                    at_least(pe, xl_kept, m + 1)
                    at_least(pe, pre_kept, m - 1)
                    high, low = w1_h[:, bass.ds(e * FF, FF)], w1_l[:, bass.ds(e * FF, FF)]
                    mm(hid_ps[b][:], x_h[:, b], high, start=True, stop=False)
                    mm(hid_ps[b][:], x_l[:, b], high, start=False, stop=False)
                    mm(hid_ps[b][:], x_h[:, b], low, start=False, stop=True).then_inc(hid_done, 1)
                m = n - LAG_R
                if is_tile(m):
                    b = (q - LAG_R) % 2
                    at_least(pe, pre_kept, m + 1)
                    at_least(pe, hidl_kept, m - 1)
                    for f in range(FC):
                        ins = nc.tensor.transpose(back_ps[b][:, f * P:(f + 1) * P], pre[:, b, f * P:(f + 1) * P], ident[:])
                    ins.then_inc(back_done, 1)
                m = n - LAG_Y
                if is_tile(m):
                    b = (q - LAG_Y) % 2
                    e = experts["now"][4 + q - LAG_Y]
                    at_least(pe, hidl_kept, m + 1)
                    at_least(pe, y_kept, m - 1)
                    weights = w2s[:].rearrange("p a h d -> p (a h d)")
                    for f in range(FC):
                        at = e * (FC * 2 * D) + f * 2 * D
                        hh, hl = hid_h[:, b, f * P:(f + 1) * P], hid_l[:, b, f * P:(f + 1) * P]
                        mm(y_ps[b][:, 0:2 * D], hh, weights[:, bass.ds(at, 2 * D)], start=f == 0, stop=False,
                           skip_group_check=True)
                        mm(y_ps[b][:, 0:D], hl, weights[:, bass.ds(at, D)], start=False, stop=False, skip_group_check=True)
                    mm(y_ps[b][:, 0:D], ones2[:], b2s[:, bass.ds(e * D, D)], start=False, stop=True,
                       skip_group_check=True).then_inc(y_done, 1)

            tiles(pe, tile)


_INS = ['x', 'L0_tok_W', 'L0_tok_b', 'L0_attn_Wq', 'L0_attn_Wk', 'L0_attn_Wv', 'L0_attn_Wlt', 'L0_ffn_Wr',
        'L0_ffn_br', 'L0_ffn_W1', 'L0_ffn_b1', 'L0_ffn_W2', 'L0_ffn_b2']


def kernel(**inputs):
    import numpy as _np
    import concourse.bacc as _bacc
    from concourse import mybir as _mybir
    from concourse.bass_utils import run_bass_kernel_spmd as _run

    nc = _bacc.Bacc("TRN2", target_bir_lowering=False, num_devices=1)
    arrays, args = {}, []
    for name in _INS:
        a = _np.ascontiguousarray(inputs[name])
        arrays[f"in_{name}_dram"] = a
        args.append(nc.dram_tensor(f"in_{name}_dram", a.shape, _mybir.dt.from_np(a.dtype), kind="ExternalInput").ap())
    args.append(nc.dram_tensor("out_0_dram", (T, D), F32, kind="ExternalOutput").ap())
    build(nc, *args)
    r = _run(nc, [arrays], core_ids=[0])
    return r.results[0]["out_0_dram"].reshape(B, S, D)
```
